# Optimizing a Trainium2 kernel written in Bass

```python
import numpy as np
import jax
import jax.numpy as jnp

def _softmax(x, axis=-1):
    return jax.nn.softmax(x, axis=axis)

def _gelu(x):
    return jax.nn.gelu(x, approximate=True)

def _silu(x):
    return jax.nn.silu(x)

def _sigmoid(x):
    return jax.nn.sigmoid(x)

def _layernorm(x, axis=-1, eps=1e-05):
    m = jnp.mean(x, axis=axis, keepdims=True)
    v = jnp.var(x, axis=axis, keepdims=True)
    return (x - m) / jnp.sqrt(v + eps)

def _scatter_add(tgt, idx, src, axis=0):
    return tgt.at[idx].add(src)

def _segment_sum(src, seg, n):
    return jax.ops.segment_sum(src, seg, n)
kernel_name = 'mk_xattn_ffn_d1_seqx_r8_520bdc'

def setup_inputs(seed: int=0):
    np.random.seed(seed)
    _w = jnp.asarray

    def _rec_inputs():
        import jax
        import jax.numpy as jnp
        _rk = jax.random.key(seed)
        x = -0.0002928 + 1 * jax.random.normal(jax.random.fold_in(_rk, 1), (8, 56, 256), jnp.float32)
        _lenS = 56 - jax.random.randint(jax.random.fold_in(_rk, 7), (8,), 0, max(1, 56 // 4) + 1, jnp.int32)
        _lenS2 = 1500 - jax.random.randint(jax.random.fold_in(_rk, 8), (8,), 0, max(1, 1500 // 4) + 1, jnp.int32)
        _ctx_512P = jax.random.normal(jax.random.fold_in(_rk, 11), (8, 16, 64), jnp.float32)
        _ctx_512c = jax.random.dirichlet(jax.random.fold_in(_rk, 511), 0.3 * jnp.ones((16,), jnp.float32), (8, 1500))
        _ctx_512t = jnp.einsum('bsk,bkd->bsd', _ctx_512c, _ctx_512P)
        _ctx_512t = _ctx_512t * jax.lax.rsqrt(jnp.mean(jnp.square(_ctx_512t)) + 1e-12) * 0.953939
        ctx_512 = 0.000227908 + 0.99994 * (_ctx_512t + 0.3 * jax.random.normal(jax.random.fold_in(_rk, 611), (8, 1500, 64), jnp.float32))
        return (x, ctx_512)
    x, ctx_512 = _rec_inputs()

    def _L0_xattn_setup():
        import jax, jax.numpy as jnp
        import numpy as np
        B, S, L = (2, 128, 128)
        DIM_Q, H, K, D_C, D_CQ, R = (256, 16, 128, 64, 192, 64)

        def _rope_tables(seq_len, dim, dtype):
            inv_freq = 1.0 / 10000.0 ** (jnp.arange(0, dim, 2, dtype=dtype) / dim)
            t = jnp.arange(seq_len, dtype=dtype)
            freqs = t[:, None] * inv_freq[None, :]
            sin = jnp.repeat(jnp.sin(freqs), 2, axis=-1)
            cos = jnp.repeat(jnp.cos(freqs), 2, axis=-1)
            return (sin, cos)

        def _rotate_half(x):
            h = x.shape[-1] // 2
            return jnp.concatenate([-x[..., h:], x[..., :h]], axis=-1)
        key = jax.random.key(seed)
        ks = jax.random.split(key, 8)
        s_in = 1.0 / np.sqrt(DIM_Q)
        s_k = 1.0 / np.sqrt(K)
        s_cq = 1.0 / np.sqrt(D_CQ)
        s_c = 1.0 / np.sqrt(D_C)
        return {'hidden_q': jax.random.normal(ks[0], (B, S, DIM_Q), jnp.float32), 'kv_c': jax.random.normal(ks[1], (B, L, D_C), jnp.float32), 'Wq': jax.random.normal(ks[2], (H * K, DIM_Q), jnp.float32) * s_in, 'w_kc_q': jax.random.normal(ks[3], (H, K, D_CQ), jnp.float32) * s_k, 'w_kc_kv': jax.random.normal(ks[4], (H, K, D_C), jnp.float32) * s_k, 'W_qr': jax.random.normal(ks[5], (H, D_CQ, R), jnp.float32) * s_cq / np.sqrt(R), 'W_kr': jax.random.normal(ks[6], (H, D_C, R), jnp.float32) * s_c, 'Wo': jax.random.normal(ks[7], (DIM_Q, H * K), jnp.float32) * s_k}
    _L0_xattn_all = _L0_xattn_setup()
    _L0_xattn_in = {k: v for k, v in _L0_xattn_all.items() if k in ('Wq', 'w_kc_q', 'w_kc_kv', 'W_qr', 'W_kr', 'Wo')}
    del _L0_xattn_all

    def _L0_ffn_setup():
        import jax, jax.numpy as jnp
        import numpy as np
        NUM_ROUTED = 7
        TOP_K = 3
        D = 256
        H = 256
        B, S = (4, 256)

        def _expert_ffn(x, w1, wg, w2):
            return jax.nn.silu(x @ w1) * (x @ wg) @ w2
        key = jax.random.key(seed)
        ks = jax.random.split(key, 8)
        s = 0.02
        return {'x': jax.random.normal(ks[0], (B, S, D), jnp.float32), 'W1': jax.random.normal(ks[1], (NUM_ROUTED, D, H), jnp.float32) * s, 'Wg': jax.random.normal(ks[2], (NUM_ROUTED, D, H), jnp.float32) * s, 'W2': jax.random.normal(ks[3], (NUM_ROUTED, H, D), jnp.float32) * s, 'Ws1': jax.random.normal(ks[4], (D, H), jnp.float32) * s, 'Wsg': jax.random.normal(ks[5], (D, H), jnp.float32) * s, 'Ws2': jax.random.normal(ks[6], (H, D), jnp.float32) * s, 'gate_w': jax.random.normal(ks[7], (D, NUM_ROUTED), jnp.float32) * s, 'gate_b': jnp.zeros((NUM_ROUTED,), jnp.float32), 'biases': jnp.zeros((NUM_ROUTED,), jnp.float32)}
    _L0_ffn_all = _L0_ffn_setup()
    _L0_ffn_in = {k: v for k, v in _L0_ffn_all.items() if k in ('W1', 'Wg', 'W2', 'Ws1', 'Wsg', 'Ws2', 'gate_w', 'gate_b', 'biases')}
    del _L0_ffn_all
    return {'x': x, 'ctx_512': ctx_512, 'L0_xattn_Wq': _L0_xattn_in['Wq'], 'L0_xattn_w_kc_q': _L0_xattn_in['w_kc_q'], 'L0_xattn_w_kc_kv': _L0_xattn_in['w_kc_kv'], 'L0_xattn_W_qr': _L0_xattn_in['W_qr'], 'L0_xattn_W_kr': _L0_xattn_in['W_kr'], 'L0_xattn_Wo': _L0_xattn_in['Wo'], 'L0_ffn_W1': _L0_ffn_in['W1'], 'L0_ffn_Wg': _L0_ffn_in['Wg'], 'L0_ffn_W2': _L0_ffn_in['W2'], 'L0_ffn_Ws1': _L0_ffn_in['Ws1'], 'L0_ffn_Wsg': _L0_ffn_in['Wsg'], 'L0_ffn_Ws2': _L0_ffn_in['Ws2'], 'L0_ffn_gate_w': _L0_ffn_in['gate_w'], 'L0_ffn_gate_b': _L0_ffn_in['gate_b'], 'L0_ffn_biases': _L0_ffn_in['biases']}

def reference(x, ctx_512, L0_xattn_Wq, L0_xattn_w_kc_q, L0_xattn_w_kc_kv, L0_xattn_W_qr, L0_xattn_W_kr, L0_xattn_Wo, L0_ffn_W1, L0_ffn_Wg, L0_ffn_W2, L0_ffn_Ws1, L0_ffn_Wsg, L0_ffn_Ws2, L0_ffn_gate_w, L0_ffn_gate_b, L0_ffn_biases):
    import jax
    import jax.numpy as jnp

    def _L0_xattn_ref(hidden_q, kv_c, Wq, w_kc_q, w_kc_kv, W_qr, W_kr, Wo):
        import jax, jax.numpy as jnp
        import numpy as np
        B, S, L = (2, 128, 128)
        DIM_Q, H, K, D_C, D_CQ, R = (256, 16, 128, 64, 192, 64)

        def _rope_tables(seq_len, dim, dtype):
            inv_freq = 1.0 / 10000.0 ** (jnp.arange(0, dim, 2, dtype=dtype) / dim)
            t = jnp.arange(seq_len, dtype=dtype)
            freqs = t[:, None] * inv_freq[None, :]
            sin = jnp.repeat(jnp.sin(freqs), 2, axis=-1)
            cos = jnp.repeat(jnp.cos(freqs), 2, axis=-1)
            return (sin, cos)

        def _rotate_half(x):
            h = x.shape[-1] // 2
            return jnp.concatenate([-x[..., h:], x[..., :h]], axis=-1)
        b, s, _ = hidden_q.shape
        l = kv_c.shape[1]
        q_hk = (hidden_q @ Wq.T).reshape(b, s, H, K)
        q_big = jnp.einsum('bshk,hkq->bshq', q_hk, w_kc_q)
        sin, cos = _rope_tables(l, D_C, kv_c.dtype)
        kv_rope = kv_c * cos[None] + _rotate_half(kv_c) * sin[None]
        q_r = jnp.einsum('bshq,hqr->bhsr', q_big, W_qr)
        k_r = jnp.einsum('bld,hdr->bhlr', kv_rope, W_kr)
        scores = jnp.einsum('bhsr,bhlr->bhsl', q_r, k_r)
        attn = jax.nn.softmax(scores, axis=-1)
        ctx_c = jnp.einsum('bhsl,bld->bhsd', attn, kv_rope)
        ctx_lat = jnp.einsum('bhsd,hkd->bshk', ctx_c, w_kc_kv)
        out = ctx_lat.reshape(b, s, H * K) @ Wo.T
        return out

    def _L0_ffn_ref(x, W1, Wg, W2, Ws1, Wsg, Ws2, gate_w, gate_b, biases):
        import jax, jax.numpy as jnp
        import numpy as np
        NUM_ROUTED = 7
        TOP_K = 3
        D = 256
        H = 256
        B, S = (4, 256)

        def _expert_ffn(x, w1, wg, w2):
            return jax.nn.silu(x @ w1) * (x @ wg) @ w2
        output = _expert_ffn(x, Ws1, Wsg, Ws2)
        gate_logits = x @ gate_w + gate_b
        gate_probas = jax.nn.softmax(gate_logits, axis=-1)
        biased_probas = gate_probas + biases
        _, topk_idxs = jax.lax.top_k(biased_probas, TOP_K)
        topk_probas = jnp.take_along_axis(gate_probas, topk_idxs, axis=-1)
        topk_probas = topk_probas / jnp.sum(topk_probas, axis=-1, keepdims=True)
        for e in range(NUM_ROUTED):
            w_e = jnp.sum(topk_probas * (topk_idxs == e), axis=-1)
            output = output + _expert_ffn(x, W1[e], Wg[e], W2[e]) * w_e[..., None]
        return output
    x = x + _L0_xattn_ref(_layernorm(x, axis=-1), ctx_512, L0_xattn_Wq, L0_xattn_w_kc_q, L0_xattn_w_kc_kv, L0_xattn_W_qr, L0_xattn_W_kr, L0_xattn_Wo)
    x = x + _L0_ffn_ref(_layernorm(x, axis=-1), L0_ffn_W1, L0_ffn_Wg, L0_ffn_W2, L0_ffn_Ws1, L0_ffn_Wsg, L0_ffn_Ws2, L0_ffn_gate_w, L0_ffn_gate_b, L0_ffn_biases)
    return x

_drawn_inputs = setup_inputs


def setup_inputs(seed=0):
    import zlib

    import numpy as np

    out = dict(_drawn_inputs(seed))
    spreads = {'L0_ffn_gate_b': (0.0, 0.8), 'L0_ffn_biases': (0.0, 0.8)}
    factors = {'L0_ffn_W1': 7.424,
     'L0_ffn_Wg': 7.385,
     'L0_ffn_W2': 7.362,
     'L0_ffn_Ws1': 4.513,
     'L0_ffn_Wsg': 4.497,
     'L0_ffn_Ws2': 4.494,
     'L0_ffn_gate_w': 8.0}
    for name, (base, spread) in spreads.items():
        noise = np.random.default_rng([zlib.crc32(name.encode()), seed]).standard_normal(out[name].shape)
        drawn = base * np.exp(spread * noise) if base else spread * noise
        out[name] = jnp.asarray(drawn.astype(out[name].dtype))
    for name, factor in factors.items():
        out[name] = (out[name] * factor).astype(out[name].dtype)
    return out
```

```python
from contextlib import ExitStack

import numpy as np

import concourse.bass as bass
from concourse import mybir

F32 = mybir.dt.float32
F16 = mybir.dt.float16
ALU = mybir.AluOpType
ACT = mybir.ActivationFunctionType
X_AXIS = mybir.AxisListType.X

BATCH, SEQ, DM = 8, 56, 256
KEYS, DC = 1500, 64
HEADS, DK, DCQ, RANK = 16, 128, 192, 64
PAIRS = HEADS // 2
TOK = BATCH * SEQ
HALF = PAIRS * SEQ
ROWS = 2 * HALF
KP, KT_N = 125, 12
STEPS = 2 * KT_N
RT = ROWS // 128
MXQ = 3
MXC = KEYS // MXQ
CHUNKS = RT * MXQ
RING = 12
TT, TP = 4, 112
EXPERTS, ROUTED, TOP_K, HID = 8, 7, 3, 256
LN_EPS = 1e-5
TAIL_AFTER = 2
QS = 16.0

POOL_TILES = [0, 2, 4, 6, 8]
DVE_TILES = [t for t in range(KT_N) if t not in POOL_TILES]
POOL_ADDS, DVE_ADDS = 2 * (len(POOL_TILES) - 1), 2 * (len(DVE_TILES) - 1)


def max_chunks_at(k):
    return [c for c in range(CHUNKS) if 3 + c * 18 // CHUNKS == k]


def adds_after(tiles, t, j):
    i = max(tiles.index(t), 1)
    return 2 * (i - 1) + j + 1


def build(nc, x, ctx, wqr, wkr, kcq, wq, kckv, wo, w_up, w_down, gate_w, gate_b, biases, before, cos, sin, out):
    es = ExitStack()
    with es:
        def sb(name, shape, dt=F32):
            return es.enter_context(nc.sbuf_tensor(name, shape, dt))

        def sem(name):
            return es.enter_context(nc.semaphore(name))

        Q_hi = sb("Q_hi", [128, BATCH * ROWS], F16)
        Q_lo = sb("Q_lo", [128, BATCH * ROWS], F16)
        K_both = [sb(f"K_both{i}", [128, KT_N, KP], F16) for i in range(2)]
        K_hi1 = [sb(f"K_hi1{i}", [128, KT_N, KP], F16) for i in range(2)]
        V = [sb(f"V{i}", [KP, KT_N, DC]) for i in range(2)]
        roped = sb("roped", [KP, KT_N, DC])
        rot = sb("rot", [KP, KT_N, DC])
        K_split = sb("K_split", [KP, KT_N, 2 * DC], F16)
        kv = sb("kv", [128, BATCH, KT_N * DC])
        cs = sb("cs", [KP, 2, KT_N * DC])
        W = sb("W", [128, 12288])
        Wq = W[:, 0:4096].rearrange("p (h d) -> p h d", h=HEADS)
        Kcq = W[0:96, 4096:8192].rearrange("p (h c k) -> p h c k", h=HEADS, c=2)
        stage_hi = W[:, 4096:5888].bitcast(F16)
        stage_lo = W[:, 5888:7680].bitcast(F16)
        WoT = W[:, 8192:12288].rearrange("p (h o) -> p h o", h=HEADS)
        Wup = W[:, 0:8192].rearrange("p (e w c h) -> p e w c h", e=EXPERTS, w=2, c=2)
        Wdn = W[:, 8192:12288].rearrange("p (e c o) -> p e c o", e=EXPERTS, c=2)
        G = sb("G", [128, 11776])
        Wqr = G[:, 0:1536].rearrange("p (n q) -> p n q", n=PAIRS)
        Wkr = G[:, 1536:2560].rearrange("p (n c) -> p n c", n=PAIRS)
        Kckv = G[:, 2560:3584].rearrange("p (h c) -> p h c", h=HEADS)
        A1 = G[0:96, 3584:5632].rearrange("p (n c d) -> p n c d", n=PAIRS, c=2)
        A2T = G[:, 5632:6656].rearrange("p (n k) -> p n k", n=PAIRS)
        A2 = G[:, 6656:7680].rearrange("p (n c) -> p n c", n=PAIRS)
        A3T = G[:, 7680:9728].rearrange("p (n d) -> p n d", n=PAIRS)
        A3 = G[:, 9728:11776].rearrange("p (n c k) -> p n c k", n=PAIRS, c=2)
        Pr = G[0:KP, 0:RING * HALF].rearrange("p (s n) -> p s n", s=RING)
        o = RING * HALF
        acc_dve = [G[0:KP, o + i * ROWS:o + (i + 1) * ROWS].rearrange("p (j n) -> p j n", j=2) for i in range(2)]
        o += 2 * ROWS
        acc_pool = [G[0:KP, o + i * ROWS:o + (i + 1) * ROWS].rearrange("p (j n) -> p j n", j=2) for i in range(2)]
        ctx_raw = sb("ctx_raw", [128, HALF])
        sums = sb("sums", [128, HALF])
        sums_thin = sb("sums_thin", [128, 7])
        recip_thin = sb("recip_thin", [128, 7])
        recip_row = sb("recip_row", [2, HALF])
        recip = sb("recip", [128, HALF])
        ctxT = sb("ctxT", [128, PAIRS, TP])
        VF = sb("VF", [128, PAIRS, DM])
        x_sb = sb("x_sb", [TP, TT, DM])
        xn = G[0:TP, 9728:10752].rearrange("p (i d) -> p i d", i=TT)
        xnT = sb("xnT", [128, 2, TOK])
        stats = sb("stats", [TP, TT, 6])
        mv = sb("mv", [TP, TT, 2])
        std = sb("std", [TP, TT])
        rstd = sb("rstd", [TP, TT])
        mx_part = sb("mx_part", [128, RT, MXQ])
        mx = sb("mx", [128, RT])
        mx16 = sb("mx16", [128, RT], F16)
        ident = sb("ident", [128, 128])
        ident16 = sb("ident16", [128, 128], F16)
        ones = sb("ones", [128, DC])
        gw = sb("gw", [128, 2, ROUTED])
        gb = sb("gb", [TP, 2, ROUTED])
        bi = sb("bi", [TP, 2, ROUTED])
        bef = sb("bef", [TP, 2, ROUTED, ROUTED])
        kvf = kv[:, :, :].rearrange("p b n -> p (b n)")
        silu_sb = kvf[:, 0:4 * TP]
        hT = [kvf[:, 448 * (i + 1):448 * (i + 2)].rearrange("p (c n) -> p c n", c=2) for i in range(2)]
        gate = {name: kvf[0:TP, 1400 + 16 * i:1414 + 16 * i].rearrange("p (i e) -> p i e", i=2)
                for i, name in enumerate(("logit", "shifted", "exp", "prob", "biased", "rank", "picked"))}
        gate1 = {name: kvf[0:TP, 1600 + 4 * i:1602 + 4 * i] for i, name in enumerate(("max", "sum", "rsum", "wsum", "rwsum"))}
        weight = kvf[0:TP, 1700:1728].rearrange("p (i e) -> p i e", i=TT)
        above, equal = (kvf[0:TP, 1800 + 100 * i:1898 + 100 * i].rearrange("p (i e f) -> p i e f", i=2, e=ROUTED) for i in range(2))

        banks = [es.enter_context(nc.psum_tensor(f"bank{i}", [128, 512], F32)) for i in range(8)]
        MX, ST, PV, AUX = banks[0:2], banks[2:5], banks[5], banks[6:8]

        in_x, in_fold1, in_fold2, in_wq, in_vfold, in_kv0, in_kvs, in_cs, in_gate, in_experts = (
            sem("in_" + n) for n in ("x", "fold1", "fold2", "wq", "vfold", "kv0", "kvs", "cs", "gate", "experts"))
        consts_ready, clear_ready = sem("consts_ready"), sem("clear_ready")
        pool_seq, dve_seq = sem("pool_seq"), sem("dve_seq")
        var_ready, std_ready, xn_ready, xt_made, xt_act, xt_dve = (
            sem(n) for n in ("var_ready", "std_ready", "xn_ready", "xt_made", "xt_act", "xt_dve"))
        fold_made, fold_act, fold_dve, q_spread0, q_spread = (
            sem(n) for n in ("fold_made", "fold_act", "fold_dve", "q_spread0", "q_spread"))
        rope_ready, k_hi_ready, k_lo_ready, kt_made, kt_ready, k_hi1_copied, v_copied = (
            sem(n) for n in ("rope_ready", "k_hi_ready", "k_lo_ready", "kt_made", "kt_ready", "k_hi1_copied", "v_copied"))
        mx_made, mx_read, mx_whole, mx16_ready, m_made, m_ready = (
            sem(n) for n in ("mx_made", "mx_read", "mx_whole", "mx16_ready", "m_made", "m_ready"))
        st_made, exp_done, pv_done, ctx_saved, dve_added, pool_added = (
            sem(n) for n in ("st_made", "exp_done", "pv_done", "ctx_saved", "dve_added", "pool_added"))
        sum_made, sum_saved, sum_thin, recip_done, recip_rowed, recip_wide, ctx_ready, proj_made, x1_ready = (
            sem(n) for n in ("sum_made", "sum_saved", "sum_thin", "recip_done", "recip_rowed", "recip_wide",
                             "ctx_ready", "proj_made", "x1_ready"))
        up_made, silu_done, h_ready, down_made, y_ready, gate_made, logits_shifted, gexp_done, w_ready, sent = (
            sem(n) for n in ("up_made", "silu_done", "h_ready", "down_made", "y_ready", "gate_made", "logits_shifted", "gexp_done",
                             "w_ready", "sent"))

        block = es.enter_context(nc.Block())

        def batches(eng, body):
            body(0, 0)
            with eng.Fori(0, 2) as n:
                body(n, 1)
                body(n, 2)
            for b in (5, 6, 7):
                body(0, b)

        def first(n, c):
            return c == 0

        def has_next(n, c):
            return c < 7

        def has_rope(n, c):
            return c < 6

        @block.sync
        def _(sp):
            sp.dma_start(Wqr, wqr).then_inc(in_fold1, 16)
            sp.wait_ge(clear_ready, 1)
            for j in range(2):
                sp.dma_start(Wkr[64 * j:64 * j + 64, :, 64 * j:64 * j + 64], wkr[64 * j:64 * j + 64]).then_inc(in_fold1, 16)
            sp.dma_start(Kcq, kcq).then_inc(in_fold2, 16)
            sp.dma_start(x_sb[:], x.rearrange("(i p) d -> p i d", p=TP)).then_inc(in_x, 16)
            sp.dma_start(kv[0:KP, 0, :], ctx[0].rearrange("(p t) c -> p (t c)", p=KP)).then_inc(in_kv0, 16)
            sp.dma_start(cs[:, 0, :], cos).then_inc(in_cs, 16)
            sp.dma_start(cs[:, 1, :], sin).then_inc(in_cs, 16)
            sp.dma_start(Wq, wq.rearrange("(h k) d -> k h d", k=DK)).then_inc(in_wq, 16)
            sp.dma_start(Kckv, kckv).then_inc(in_vfold, 16)
            sp.dma_start(WoT, wo).then_inc(in_vfold, 16)
            for b in range(1, BATCH):
                sp.dma_start(kv[0:KP, b, :], ctx[b].rearrange("(p t) c -> p (t c)", p=KP)).then_inc(in_kvs, 16)
            sp.dma_start(gw[:], gate_w).then_inc(in_gate, 16)
            sp.dma_start(gb[:], gate_b).then_inc(in_gate, 16)
            sp.dma_start(bi[:], biases).then_inc(in_gate, 16)
            sp.dma_start(bef[:], before).then_inc(in_gate, 16)

            def copy_v(n, c):
                b = 2 * n + c
                sp.wait_ge(rope_ready, b + 1)
                if c >= 2:
                    sp.wait_ge(pv_done, KT_N * (b - 1))
                sp.dma_start(V[c % 2][:], roped[:]).then_inc(v_copied, 16)

            def copy_k(n, c):
                b = 2 * n + c
                sp.wait_ge(kt_ready, 2 * (b + 1))
                sp.dma_start(K_hi1[c % 2][0:64], K_both[c % 2][0:64]).then_inc(k_hi1_copied, 16)

            copy_v(0, 0)
            for lo, hi in ((0, 1), (1, BATCH)):
                nb = hi - lo
                Qh = Q_hi[:, lo * ROWS:hi * ROWS].rearrange("p (b j n) -> p b j n", b=nb, j=2)
                Ql = Q_lo[:, lo * ROWS:hi * ROWS].rearrange("p (b j n) -> p b j n", b=nb, j=2)
                Sh = stage_hi[:, lo * HALF:hi * HALF].rearrange("p (b n) -> p b n", b=nb)
                Sl = stage_lo[:, lo * HALF:hi * HALF].rearrange("p (b n) -> p b n", b=nb)
                spread = q_spread0 if lo == 0 else q_spread
                if lo == 0:
                    sp.wait_ge(fold_act, 20 + PAIRS)
                for j in range(2):
                    for to in range(2):
                        sp.dma_start(Qh[64 * to:64 * to + 64, :, j], Sh[64 * j:64 * j + 64]).then_inc(spread, 16)
                if lo == 0:
                    sp.wait_ge(fold_dve, 20 + PAIRS)
                    sp.wait_ge(clear_ready, 2)
                for j in range(2):
                    sp.dma_start(Ql[0:64, :, j], Sl[64 * j:64 * j + 64]).then_inc(spread, 16)
            copy_k(0, 0)
            sp.wait_ge(q_spread0, 6 * 16)
            sp.wait_ge(q_spread, 6 * 16)
            sp.wait_ge(fold_act, 20 + PAIRS + PAIRS // 2)
            sp.wait_ge(fold_dve, 20 + PAIRS + PAIRS // 2)
            sp.dma_start(Wup, w_up).then_inc(in_experts, 16)
            sp.dma_start(Wdn, w_down).then_inc(in_experts, 16)

            def normaliser(n, c):
                b = 2 * n + c
                sp.wait_ge(sum_saved, b + 1)
                for j in range(2):
                    sp.dma_start(sums_thin[64 * j:64 * j + 64, :], sums[64 * j:64 * j + 1, :]).then_inc(sum_thin, 16)
                sp.wait_ge(recip_done, b + 1)
                for j in range(2):
                    sp.dma_start(recip_row[j:j + 1, :], recip_thin[64 * j:64 * j + 64, :]).then_inc(recip_rowed, 16)
                sp.wait_ge(recip_rowed, 32 * (b + 1))
                for j in range(2):
                    sp.dma_start(recip[64 * j:64 * j + 64, :],
                                 recip_row[j:j + 1, :].unsqueeze(1).to_broadcast([1, 64, HALF])).then_inc(recip_wide, 16)

            def body(n, c):
                if has_next(n, c):
                    copy_v(n, c + 1)
                    copy_k(n, c + 1)
                if not first(n, c):
                    normaliser(n, c - 1)

            batches(sp, body)
            normaliser(0, 7)
            for g in range(2):
                sp.wait_ge(y_ready, 2 * EXPERTS * (g + 1))
                sp.dma_start(out.rearrange("(i p) d -> p i d", p=TP)[:, 2 * g:2 * g + 2], x_sb[:, 2 * g:2 * g + 2, :]).then_inc(sent, 16)
            sp.wait_ge(sent, 32)

        @block.gpsimd
        def _(pool):
            nc.gpsimd.memset(Wkr, 0.0).then_inc(clear_ready, 1)
            nc.gpsimd.memset(ident[:], 0.0)
            nc.gpsimd.memset(ident16[:], 0.0)
            nc.gpsimd.memset(ones[:], 1.0).then_inc(pool_seq, 1)
            pool.wait_ge(pool_seq, 1)
            for m in (ident, ident16):
                last = nc.gpsimd.affine_select(out=m[:], in_=m[:], compare_op=ALU.not_equal, fill=1.0, base=0,
                                               pattern=[[-1, 128]], channel_multiplier=1)
            last.then_inc(consts_ready, 1)
            pool.wait_ge(consts_ready, 1)
            for i in range(2):
                nc.gpsimd.memset(K_hi1[i][64:128], 0.0)
            nc.gpsimd.memset(Q_lo[64:128, :].bitcast(F32), 0.0).then_inc(clear_ready, 1)
            pool.wait_ge(clear_ready, 2)
            for i in range(2):
                last = nc.gpsimd.memset(K_hi1[i][64:65], -QS)
            last.then_inc(consts_ready, 1)
            pool.wait_ge(consts_ready, 2)

            def rope(n, c):
                b = 2 * n + c
                raw = kvf[0:KP, bass.ds(b * (KT_N * DC), KT_N * DC)].rearrange("p (t c) -> p t c", c=DC)
                cosv, sinv = (cs[:, i, :].rearrange("p (t c) -> p t c", c=DC) for i in range(2))
                if c >= 1:
                    pool.wait_ge(v_copied, 16 * b)
                    pool.wait_ge(k_lo_ready, b)
                nc.gpsimd.tensor_tensor(roped[:], raw, cosv, ALU.mult)
                h = DC // 2
                nc.gpsimd.tensor_tensor(rot[:, :, 0:h], raw[:, :, h:DC], sinv[:, :, 0:h], ALU.mult)
                nc.gpsimd.tensor_tensor(rot[:, :, h:DC], raw[:, :, 0:h], sinv[:, :, h:DC], ALU.mult).then_inc(pool_seq, 1)
                pool.wait_ge(pool_seq, 2 + b)
                nc.gpsimd.tensor_tensor(roped[:], roped[:], rot[:], ALU.add).then_inc(rope_ready, 1)

            def low(n, c):
                b = 2 * n + c
                pool.wait_ge(k_hi_ready, b + 1)
                nc.gpsimd.tensor_tensor(K_split[:, :, DC:2 * DC], roped[:], K_split[:, :, 0:DC], ALU.subtract)\
                    .then_inc(k_lo_ready, 1)

            def add(n, c, i, j):
                b = 2 * n + c
                t = POOL_TILES[i]
                pool.wait_ge(exp_done, STEPS * b + 2 * t + j + 1)
                to = acc_pool[c % 2][:, j, :]
                if i == 1:
                    a = Pr[:, (2 * POOL_TILES[0] + j) % RING, :]
                else:
                    a = to
                    pool.wait_ge(pool_added, POOL_ADDS * b + 2 * (i - 1) + j - 1)
                nc.gpsimd.tensor_tensor(to, a, Pr[:, (2 * t + j) % RING, :], ALU.add).then_inc(pool_added, 1)

            pool.wait_ge(in_cs, 32)
            pool.wait_ge(in_kv0, 16)
            rope(0, 0)
            low(0, 0)
            pool.wait_ge(in_kvs, 16 * (BATCH - 1))
            rope(0, 1)
            low(0, 1)

            def body(n, c):
                for j in range(2):
                    add(n, c, 1, j)
                if has_rope(n, c):
                    rope(n, c + 2)
                for i in range(2, len(POOL_TILES)):
                    for j in range(2):
                        add(n, c, i, j)
                if has_rope(n, c):
                    low(n, c + 2)

            batches(pool, body)


        @block.scalar
        def _(act):
            def copy(to, of, **k):
                return nc.scalar.activation(to, of, ACT.Copy, **k)

            def k_hi(n, c):
                b = 2 * n + c
                act.wait_ge(rope_ready, b + 1)
                if c >= 1:
                    act.wait_ge(kt_made, 2 * b)
                copy(K_split[:, :, 0:DC], roped[:]).then_inc(k_hi_ready, 1)

            def kt(n, c, i):
                b = 2 * n + c
                act.wait_ge(kt_made, 2 * b + i + 1)
                of = AUX[i][:, :].bitcast(F16).rearrange("p (t k) -> p t k", k=128)[:, 0:6, 0:KP]
                copy(K_both[c % 2][:, 6 * i:6 * i + 6, :], of).then_inc(kt_ready, 1)

            def m_rows(n, c):
                b = 2 * n + c
                for j in range(2):
                    act.wait_ge(m_made, 2 * b + j + 1)
                    copy(Q_lo[64:65, bass.ds(b * ROWS + j * HALF, HALF)], AUX[j][64:65, 0:HALF]).then_inc(m_ready, 1)

            def save_ctx(n, c):
                b = 2 * n + c
                act.wait_ge(pv_done, KT_N * (b + 1))
                if c >= 1:
                    act.wait_ge(ctx_ready, b)
                copy(ctx_raw[:], PV[:, 0:HALF]).then_inc(ctx_saved, 1)

            def save_sums(n, c):
                b = 2 * n + c
                act.wait_ge(sum_made, b + 1)
                if c >= 1:
                    act.wait_ge(sum_thin, 32 * b)
                copy(sums[:], AUX[0][:, 0:HALF]).then_inc(sum_saved, 1)

            act.wait_ge(var_ready, 1)
            nc.scalar.activation(std[:], rstd[:], ACT.Sqrt).then_inc(std_ready, 1)
            nc.scalar.preload_act_table(ACT.Exp)

            fold_to = [lambda p: (A1[:, p], banks[p][0:96, 0:256]), lambda p: (A2T[:, p], banks[p][:, 0:128]),
                       lambda p: (A2[:, p], banks[p][:, 0:128]), lambda p: (A3T[:, p], banks[p][:, 0:256]),
                       lambda p: (A3[:, p], banks[p][:, 0:256])]
            for s in range(5):
                for p in range(0, PAIRS, 2):
                    act.wait_ge(fold_made, PAIRS * s + p + 1)
                    to, of = fold_to[s](p)
                    if len(to.shape) == 3:
                        of = of.rearrange("p (c n) -> p c n", c=2)
                    copy(to, of).then_inc(fold_act, 1)
                if s == 2:
                    for i in (0, 2):
                        act.wait_ge(xt_made, i + 1)
                        copy(xnT[:, :, TP * i:TP * i + TP], banks[i][:, 0:2 * TP].rearrange("p (c n) -> p c n", c=2))\
                            .then_inc(xt_act, 1)
            k_hi(0, 0)
            for p in range(PAIRS):
                act.wait_ge(fold_made, 5 * PAIRS + p + 1)
                copy(stage_hi.rearrange("q (b n) -> q b n", b=BATCH)[:, :, SEQ * p:SEQ * p + SEQ],
                     banks[p][:, 0:TOK].rearrange("q (b s) -> q b s", b=BATCH), scale=QS).then_inc(fold_act, 1)
            for p in range(0, PAIRS, 2):
                act.wait_ge(fold_made, 6 * PAIRS + p + 1)
                copy(VF[:, p], banks[p][:, 0:DM]).then_inc(fold_act, 1)
            for i in range(2):
                kt(0, 0, i)
            k_hi(0, 1)
            m_rows(0, 0)

            def body(n, c):
                b = 2 * n + c
                for k in range(STEPS):
                    act.wait_ge(st_made, STEPS * b + k + 1)
                    if not (first(n, c) and k < RING):
                        bb, kk = (b, k - RING) if k >= RING else (b - 1, k - RING + STEPS)
                        act.wait_ge(pv_done, KT_N * bb + kk // 2 + 1)
                        t, j = kk // 2, kk % 2
                        if t in POOL_TILES:
                            act.wait_ge(pool_added, POOL_ADDS * bb + adds_after(POOL_TILES, t, j))
                        else:
                            act.wait_ge(dve_added, DVE_ADDS * bb + adds_after(DVE_TILES, t, j))
                    nc.scalar.activation(Pr[:, k % RING, :], ST[k % 3][0:KP, 0:HALF], ACT.Exp, scale=1.0 / QS)\
                        .then_inc(exp_done, 1)
                    if k < 2 and has_next(n, c):
                        kt(n, c + 1, k)
                    if k == 2 and not first(n, c):
                        save_ctx(n, c - 1)
                    if k == 5 and not first(n, c):
                        save_sums(n, c - 1)
                    if k == 12 and has_rope(n, c):
                        k_hi(n, c + 2)
                if has_next(n, c):
                    m_rows(n, c + 1)

            batches(act, body)
            save_ctx(0, 7)
            save_sums(0, 7)

            def norm(g):
                act.wait_ge(var_ready, g + 2)
                nc.scalar.activation(std[:, 2 * g:2 * g + 2], rstd[:, 2 * g:2 * g + 2], ACT.Sqrt).then_inc(std_ready, 1)

            def spread_x(g):
                act.wait_ge(xt_made, TT + g + 1)
                for i in range(2):
                    last = copy(xnT[:, :, TP * (2 * g + i):TP * (2 * g + i + 1)],
                                banks[6][:, 2 * TP * i:2 * TP * (i + 1)].rearrange("p (c n) -> p c n", c=2))
                last.then_inc(xt_act, 1)

            def gate_exp(g):
                act.wait_ge(logits_shifted, g + 1)
                nc.scalar.activation(gate["exp"], gate["shifted"], ACT.Exp).then_inc(gexp_done, 1)

            norm(0)
            for u in range(2 * EXPERTS):
                if u % EXPERTS == 0:
                    spread_x(u // EXPERTS)
                    gate_exp(u // EXPERTS)
                act.wait_ge(up_made, u + 1)
                if u >= 1:
                    act.wait_ge(h_ready, u)
                nc.scalar.activation(silu_sb, banks[2 * (u % 2)][:, 0:4 * TP], ACT.Silu).then_inc(silu_done, 1)
                if u == TAIL_AFTER:
                    norm(1)

        @block.vector
        def _(dve):
            chain = [0]

            def link(ins):
                chain[0] += 1
                ins.then_inc(dve_seq, 1)
                dve.wait_ge(dve_seq, chain[0])

            def norm(tiles, k):
                lo, hi = tiles[0], tiles[-1] + 1
                for i in tiles:
                    last = nc.vector.bn_stats(stats[:, i, :], x_sb[:, i, :])
                link(last)
                for i in tiles:
                    last = nc.vector.bn_aggr(mv[:, i, :], stats[:, i, :])
                link(last)
                nc.vector.tensor_scalar(rstd[:, lo:hi], mv[:, lo:hi, 1], LN_EPS, None, ALU.add).then_inc(var_ready, 1)

            def normalise(tiles, k):
                lo, hi = tiles[0], tiles[-1] + 1
                dve.wait_ge(std_ready, k + 1)
                link(nc.vector.reciprocal(rstd[:, lo:hi], std[:, lo:hi]))
                for i in tiles:
                    last = nc.vector.tensor_scalar(xn[:, i, :], x_sb[:, i, :], mv[:, i, 0:1], rstd[:, i:i + 1],
                                                   ALU.subtract, ALU.mult)
                last.then_inc(xn_ready, 1)

            dve.wait_ge(in_x, 16)
            norm(range(TT), 0)
            normalise(range(TT), 0)

            fold_to = [lambda p: (A1[:, p], banks[p][0:96, 0:256]), lambda p: (A2T[:, p], banks[p][:, 0:128]),
                       lambda p: (A2[:, p], banks[p][:, 0:128]), lambda p: (A3T[:, p], banks[p][:, 0:256]),
                       lambda p: (A3[:, p], banks[p][:, 0:256])]
            for s in range(5):
                for p in range(1, PAIRS, 2):
                    dve.wait_ge(fold_made, PAIRS * s + p + 1)
                    to, of = fold_to[s](p)
                    if len(to.shape) == 3:
                        of = of.rearrange("p (c n) -> p c n", c=2)
                    nc.vector.tensor_copy(to, of).then_inc(fold_dve, 1)
                if s == 2:
                    for i in (1, 3):
                        dve.wait_ge(xt_made, i + 1)
                        nc.vector.tensor_copy(xnT[:, :, TP * i:TP * i + TP],
                                              banks[i][:, 0:2 * TP].rearrange("p (c n) -> p c n", c=2)).then_inc(xt_dve, 1)
            for p in range(PAIRS):
                dve.wait_ge(fold_act, 20 + p + 1)
                part = slice(SEQ * p, SEQ * p + SEQ)
                nc.vector.scalar_tensor_tensor(
                    stage_lo.rearrange("q (b n) -> q b n", b=BATCH)[:, :, part],
                    banks[p][:, 0:TOK].rearrange("q (b s) -> q b s", b=BATCH), QS,
                    stage_hi.rearrange("q (b n) -> q b n", b=BATCH)[:, :, part], ALU.mult, ALU.subtract).then_inc(fold_dve, 1)
            for p in range(1, PAIRS, 2):
                dve.wait_ge(fold_made, 6 * PAIRS + p + 1)
                nc.vector.tensor_copy(VF[:, p], banks[p][:, 0:DM]).then_inc(fold_dve, 1)

            def reduce_chunk(n, c, i):
                b = 2 * n + c
                dve.wait_ge(mx_made, CHUNKS * b + i + 1)
                nc.vector.tensor_reduce(mx_part[:, i // MXQ, i % MXQ:i % MXQ + 1], MX[(c + i) % 2][:, 0:MXC],
                                        X_AXIS, ALU.max).then_inc(mx_read, 1)

            def maxima(n, c):
                b = 2 * n + c
                dve.wait_ge(mx_read, CHUNKS * (b + 1))
                nc.vector.tensor_reduce(mx[:], mx_part[:], X_AXIS, ALU.max).then_inc(mx_whole, 1)
                dve.wait_ge(mx_whole, b + 1)
                nc.vector.tensor_scalar(mx16[:], mx[:], 1.0 / QS, None, ALU.mult).then_inc(mx16_ready, 1)

            def add(n, c, t, j):
                b = 2 * n + c
                i = DVE_TILES.index(t)
                if i == 0:
                    return
                dve.wait_ge(exp_done, STEPS * b + 2 * t + j + 1)
                to = acc_dve[c % 2][:, j, :]
                if i == 1:
                    a = Pr[:, (2 * DVE_TILES[0] + j) % RING, :]
                else:
                    a = to
                    dve.wait_ge(dve_added, DVE_ADDS * b + 2 * (i - 1) + j - 1)
                nc.vector.tensor_tensor(to, a, Pr[:, (2 * t + j) % RING, :], ALU.add).then_inc(dve_added, 1)

            def reciprocals(n, c):
                b = 2 * n + c
                dve.wait_ge(sum_thin, 32 * (b + 1))
                nc.vector.reciprocal(recip_thin[:], sums_thin[:]).then_inc(recip_done, 1)

            def context(n, c):
                b = 2 * n + c
                dve.wait_ge(recip_wide, 32 * (b + 1))
                dve.wait_ge(ctx_saved, b + 1)
                at = SEQ * (c % 2)
                nc.vector.tensor_tensor(ctxT[:, :, at:at + SEQ], ctx_raw[:].rearrange("p (h s) -> p h s", h=PAIRS),
                                        recip[:].rearrange("p (h s) -> p h s", h=PAIRS), ALU.mult).then_inc(ctx_ready, 1)

            def residual(tile):
                dve.wait_ge(proj_made, tile + 1)
                at = x_flat[:, bass.ds(tile * DM, DM)]
                nc.vector.tensor_tensor(at, AUX[1][0:TP, 0:DM], at, ALU.add).then_inc(x1_ready, 1)

            x_flat = x_sb[:, :, :].rearrange("p i d -> p (i d)")
            for i in range(CHUNKS):
                reduce_chunk(0, 0, i)
            maxima(0, 0)

            def body(n, c):
                for k in range(STEPS + 2):
                    if has_next(n, c):
                        for i in max_chunks_at(k):
                            reduce_chunk(n, c + 1, i)
                    if k >= 2 and (k - 2) // 2 in DVE_TILES:
                        add(n, c, (k - 2) // 2, k % 2)
                    if k == 9 and not first(n, c):
                        reciprocals(n, c - 1)
                    if k == 15 and not first(n, c):
                        context(n, c - 1)
                    if k == 19 and c % 2 == 0 and not first(n, c):
                        residual(n + c // 2 - 1)
                    if k == 20 and has_next(n, c):
                        maxima(n, c + 1)

            batches(dve, body)

            def gating(g):
                dve.wait_ge(gate_made, g + 1)
                logit = banks[7][0:TP, 0:32].rearrange("p (i e) -> p i e", i=2)[:, :, 0:ROUTED]
                wide = lambda v: v.unsqueeze(2).to_broadcast([TP, 2, ROUTED])
                link(nc.vector.tensor_tensor(gate["logit"], logit, gb[:], ALU.add))
                link(nc.vector.tensor_reduce(gate1["max"], gate["logit"], X_AXIS, ALU.max))
                nc.vector.tensor_tensor(gate["shifted"], gate["logit"], wide(gate1["max"]), ALU.subtract).then_inc(logits_shifted, 1)
                dve.wait_ge(gexp_done, g + 1)
                link(nc.vector.tensor_reduce(gate1["sum"], gate["exp"], X_AXIS, ALU.add))
                link(nc.vector.reciprocal(gate1["rsum"], gate1["sum"]))
                link(nc.vector.tensor_tensor(gate["prob"], gate["exp"], wide(gate1["rsum"]), ALU.mult))
                link(nc.vector.tensor_tensor(gate["biased"], gate["prob"], bi[:], ALU.add))
                other = gate["biased"].unsqueeze(2).to_broadcast([TP, 2, ROUTED, ROUTED])
                own = gate["biased"].unsqueeze(3).to_broadcast([TP, 2, ROUTED, ROUTED])
                nc.vector.tensor_tensor(above, other, own, ALU.is_gt)
                link(nc.vector.tensor_tensor(equal, other, own, ALU.is_equal))
                link(nc.vector.tensor_tensor(equal, equal, bef[:], ALU.mult))
                link(nc.vector.tensor_tensor(above, above, equal, ALU.add))
                link(nc.vector.tensor_reduce(gate["rank"], above, X_AXIS, ALU.add))
                link(nc.vector.tensor_scalar(gate["rank"], gate["rank"], TOP_K - 0.5, None, ALU.is_lt))
                link(nc.vector.tensor_tensor(gate["picked"], gate["prob"], gate["rank"], ALU.mult))
                link(nc.vector.tensor_reduce(gate1["wsum"], gate["picked"], X_AXIS, ALU.add))
                link(nc.vector.reciprocal(gate1["rwsum"], gate1["wsum"]))
                link(nc.vector.tensor_tensor(weight[:, 2 * g:2 * g + 2], gate["picked"], wide(gate1["rwsum"]), ALU.mult))

            def combine(u):
                g, e = divmod(u, EXPERTS)
                dve.wait_ge(down_made, u + 1)
                for i in range(2):
                    t = 2 * g + i
                    of = banks[4 + u % 2][0:TP, DM * i:DM * i + DM]
                    if e == 0:
                        nc.vector.tensor_tensor(x_sb[:, t, :], of, x_sb[:, t, :], ALU.add).then_inc(y_ready, 1)
                    else:
                        dve.wait_ge(y_ready, 2 * (u - 1) + i + 1)
                        nc.vector.scalar_tensor_tensor(x_sb[:, t, :], of, weight[:, t, e - 1:e], x_sb[:, t, :],
                                                       ALU.mult, ALU.add).then_inc(y_ready, 1)

            dve.wait_ge(x1_ready, 2)
            norm((0, 1), 1)
            reciprocals(0, 7)
            normalise((0, 1), 1)
            context(0, 7)
            for u in range(2 * EXPERTS):
                if u % EXPERTS == 0:
                    gating(u // EXPERTS)
                dve.wait_ge(silu_done, u + 1)
                if u >= 2:
                    dve.wait_ge(down_made, u - 1)
                nc.vector.tensor_tensor(hT[u % 2].rearrange("p c n -> p (c n)"), silu_sb, banks[2 * (u % 2) + 1][:, 0:4 * TP],
                                        ALU.mult).then_inc(h_ready, 1)
                if u >= 1:
                    combine(u - 1)
                if u == TAIL_AFTER:
                    residual(TT - 1)
                    dve.wait_ge(x1_ready, TT)
                    norm((2, 3), 2)
                    normalise((2, 3), 2)
            combine(2 * EXPERTS - 1)

        @block.tensor
        def _(pe):
            def folded(s, p):
                pe.wait_ge(fold_act if p % 2 == 0 else fold_dve, 4 * s + p // 2 + 1)

            pe.wait_ge(consts_ready, 1)
            pe.wait_ge(in_fold1, 48)
            for p in range(PAIRS):
                for c in range(2):
                    last = nc.tensor.matmul(banks[p][0:96, 128 * c:128 * c + 128], Wqr[:, p, 96 * c:96 * c + 96],
                                            Wkr[:, p, :], start=True, stop=True)
                last.then_inc(fold_made, 1)
            pe.wait_ge(in_fold2, 16)
            for p in range(PAIRS):
                folded(0, p)
                for c in range(2):
                    for j in range(2):
                        last = nc.tensor.matmul(banks[p][64 * j:64 * j + 64, 0:128], A1[:, p, c, 64 * j:64 * j + 64],
                                                Kcq[:, p + PAIRS * j, c, :], start=(c == 0), stop=(c == 1))
                last.then_inc(fold_made, 1)
            for p in range(PAIRS):
                folded(1, p)
                nc.tensor.transpose(banks[p][:, 0:128], A2T[:, p, :], ident[:]).then_inc(fold_made, 1)
            pe.wait_ge(xn_ready, 1)
            for i in range(TT):
                folded(2, i)
                for c in range(2):
                    last = nc.tensor.transpose(banks[i][:, TP * c:TP * c + TP], xn[:, i, 128 * c:128 * c + 128],
                                               ident[0:TP, 0:TP])
                last.then_inc(xt_made, 1)
            pe.wait_ge(in_wq, 16)
            for p in range(PAIRS):
                folded(2, p)
                if p < TT:
                    pe.wait_ge(xt_act if p % 2 == 0 else xt_dve, p // 2 + 1)
                for j in range(2):
                    last = nc.tensor.matmul(banks[p][64 * j:64 * j + 64, 0:DM], A2[:, p, 64 * j:64 * j + 64],
                                            Wq[:, p + PAIRS * j, :], start=True, stop=True)
                last.then_inc(fold_made, 1)
            for p in range(PAIRS):
                folded(3, p)
                for c in range(2):
                    last = nc.tensor.transpose(banks[p][:, 128 * c:128 * c + 128], A3T[:, p, 128 * c:128 * c + 128], ident[:])
                last.then_inc(fold_made, 1)
            for p in range(PAIRS):
                folded(4, p)
                for c in range(2):
                    last = nc.tensor.matmul(banks[p][:, 0:TOK], A3[:, p, c, :], xnT[:, c, :], start=(c == 0), stop=(c == 1))
                last.then_inc(fold_made, 1)
            pe.wait_ge(in_vfold, 32)
            for p in range(PAIRS):
                pe.wait_ge(fold_dve, 20 + p + 1)
                for j in range(2):
                    last = nc.tensor.matmul(banks[p][64 * j:64 * j + 64, 0:DM], Kckv[:, p + PAIRS * j, :],
                                            WoT[:, p + PAIRS * j, :], start=True, stop=True)
                last.then_inc(fold_made, 1)

            def kt(n, c):
                b = 2 * n + c
                pe.wait_ge(k_lo_ready, b + 1)
                for t in range(KT_N):
                    to = AUX[t // 6][:, :].bitcast(F16)[:, 128 * (t % 6):128 * (t % 6) + KP]
                    last = nc.tensor.transpose(to, K_split[:, t, :], ident16[0:KP, 0:KP])
                    if t % 6 == 5:
                        last.then_inc(kt_made, 1)

            def max_chunk(n, c, i):
                b = 2 * n + c
                if i == 0:
                    pe.wait_ge(kt_ready, 2 * (b + 1))
                if not (c == 0 and i < 2):
                    pe.wait_ge(mx_read, CHUNKS * b + i - 1)
                r, q = divmod(i, MXQ)
                nc.tensor.matmul(MX[(c + i) % 2][:, 0:MXC], Q_hi[:, bass.ds(b * ROWS + 128 * r, 128)],
                                 K_both[c % 2][:, 4 * q:4 * q + 4, :].rearrange("p t k -> p (t k)"),
                                 start=True, stop=True).then_inc(mx_made, 1)

            def m_row(n, c):
                b = 2 * n + c
                pe.wait_ge(mx16_ready, b + 1)
                for j in range(2):
                    for r in range(RT):
                        lo, hi = max(128 * r, HALF * j), min(128 * r + 128, HALF * j + HALF)
                        if lo < hi:
                            last = nc.tensor.matmul(AUX[j][64:65, lo - HALF * j:hi - HALF * j], mx16[:, r:r + 1],
                                                    ident16[:, lo - 128 * r:hi - 128 * r], start=True, stop=True)
                    last.then_inc(m_made, 1)

            def pv(n, c, t):
                b = 2 * n + c
                pe.wait_ge(exp_done, STEPS * b + 2 * t + 2)
                if t == 0:
                    pe.wait_ge(v_copied, 16 * (b + 1))
                    if c >= 1:
                        pe.wait_ge(ctx_saved, b)
                for j in range(2):
                    last = nc.tensor.matmul(PV[64 * j:64 * j + 64, 0:HALF], V[c % 2][:, t, :], Pr[:, (2 * t + j) % RING, :],
                                            start=(t == 0), stop=(t == KT_N - 1))
                last.then_inc(pv_done, 1)

            def row_sums(n, c):
                b = 2 * n + c
                pe.wait_ge(dve_added, DVE_ADDS * (b + 1))
                pe.wait_ge(pool_added, POOL_ADDS * (b + 1))
                for a in (acc_dve, acc_pool):
                    for j in range(2):
                        last = nc.tensor.matmul(AUX[0][64 * j:64 * j + 64, 0:HALF], ones[0:KP, :], a[c % 2][:, j, :],
                                                start=(a is acc_dve), stop=(a is acc_pool))
                last.then_inc(sum_made, 1)

            def project(n, c, parts):
                b = 2 * n + c
                if parts[0] == 0:
                    pe.wait_ge(ctx_ready, b + 1)
                for p in parts:
                    last = nc.tensor.matmul(AUX[1][0:TP, 0:DM], ctxT[:, p, :], VF[:, p, :], start=(p == 0), stop=(p == PAIRS - 1))
                if parts[-1] == PAIRS - 1:
                    last.then_inc(proj_made, 1)

            pe.wait_ge(fold_act, 28 + PAIRS // 2)
            pe.wait_ge(fold_dve, 28 + PAIRS // 2)
            kt(0, 0)
            pe.wait_ge(q_spread0, 6 * 16)
            for i in range(CHUNKS):
                max_chunk(0, 0, i)
            m_row(0, 0)
            pe.wait_ge(consts_ready, 2)

            def body(n, c):
                b = 2 * n + c
                for k in range(STEPS):
                    t, j = divmod(k, 2)
                    rows = bass.ds(b * ROWS + HALF * j, HALF)
                    if k == 0:
                        pe.wait_ge(m_ready, 2 * (b + 1))
                        pe.wait_ge(k_hi1_copied, 16 * (b + 1))
                    if not (first(n, c) and k < 3):
                        pe.wait_ge(exp_done, STEPS * b + k - 2)
                    nc.tensor.matmul(ST[k % 3][0:KP, 0:HALF], K_both[c % 2][:, t, :], Q_hi[:, rows], start=True, stop=False)
                    nc.tensor.matmul(ST[k % 3][0:KP, 0:HALF], K_hi1[c % 2][:, t, :], Q_lo[:, rows], start=False, stop=True)\
                        .then_inc(st_made, 1)
                    if first(n, c) and k == 0:
                        pe.wait_ge(q_spread, 6 * 16)
                    if has_next(n, c):
                        if k == 0:
                            kt(n, c + 1)
                        for i in max_chunks_at(k):
                            max_chunk(n, c + 1, i)
                    if k == 1 and not first(n, c):
                        pv(n, c - 1, KT_N - 1)
                    if j == 1 and t >= 1:
                        pv(n, c, t - 1)
                    if k == 4 and not first(n, c):
                        if has_next(n, c):
                            pe.wait_ge(kt_ready, 2 * (b + 2))
                        row_sums(n, c - 1)
                    if 16 <= k < 20 and c % 2 == 0 and not first(n, c):
                        project(n, c - 1, (2 * (k - 16), 2 * (k - 16) + 1))
                    if k == 22 and has_next(n, c):
                        if not first(n, c):
                            pe.wait_ge(sum_saved, b)
                        m_row(n, c + 1)

            batches(pe, body)
            pv(0, 7, KT_N - 1)
            row_sums(0, 7)

            def tokens(g):
                pe.wait_ge(xn_ready, g + 2)
                pe.wait_ge(sum_saved, BATCH)
                for i in range(2):
                    for c in range(2):
                        last = nc.tensor.transpose(banks[6][:, TP * (2 * i + c):TP * (2 * i + c) + TP],
                                                   xn[:, 2 * g + i, 128 * c:128 * c + 128], ident[0:TP, 0:TP])
                last.then_inc(xt_made, 1)
                pe.wait_ge(xt_act, 2 + g + 1)
                if g == 1:
                    pe.wait_ge(x1_ready, TT)
                for i in range(2):
                    for c in range(2):
                        last = nc.tensor.matmul(banks[7][0:TP, 16 * i:16 * i + ROUTED],
                                                xnT[:, c, TP * (2 * g + i):TP * (2 * g + i + 1)], gw[:, c, :],
                                                start=(c == 0), stop=(c == 1))
                last.then_inc(gate_made, 1)

            def up(u):
                g, e = divmod(u, EXPERTS)
                if u >= 2:
                    pe.wait_ge(h_ready, u - 1)
                for w in range(2):
                    for h in range(2):
                        for c in range(2):
                            last = nc.tensor.matmul(banks[2 * (u % 2) + w][:, 2 * TP * h:2 * TP * (h + 1)],
                                                    Wup[:, e, w, c, 128 * h:128 * h + 128],
                                                    xnT[:, c, 2 * TP * g:2 * TP * (g + 1)], start=(c == 0), stop=(c == 1))
                last.then_inc(up_made, 1)

            def down(u):
                g, e = divmod(u, EXPERTS)
                pe.wait_ge(h_ready, u + 1)
                if u >= 2:
                    pe.wait_ge(y_ready, 2 * (u - 1))
                for i in range(2):
                    for c in range(2):
                        last = nc.tensor.matmul(banks[4 + u % 2][0:TP, DM * i:DM * i + DM],
                                                hT[u % 2][:, c, TP * i:TP * i + TP], Wdn[:, e, c, :],
                                                start=(c == 0), stop=(c == 1))
                last.then_inc(down_made, 1)

            pe.wait_ge(in_gate, 64)
            tokens(0)
            pe.wait_ge(in_experts, 32)
            up(0)
            for u in range(2 * EXPERTS):
                if u == TAIL_AFTER:
                    project(0, 7, range(PAIRS))
                if u == EXPERTS - 1:
                    tokens(1)
                if u + 1 < 2 * EXPERTS:
                    up(u + 1)
                down(u)


def rotary_tables():
    inv_freq = np.float32(1.0) / np.float32(10000.0) ** (np.arange(0, DC, 2, dtype=np.float32) / np.float32(DC))
    angle = np.arange(KEYS, dtype=np.float32)[:, None] * inv_freq[None, :]
    sin, cos = (np.repeat(f(angle), 2, axis=-1).astype(np.float32) for f in (np.sin, np.cos))
    sin[:, :DC // 2] *= -1
    return [np.ascontiguousarray(a.reshape(KP, KT_N * DC)) for a in (cos, sin)]


def kernel(**inputs):
    import concourse.bacc as bacc
    from concourse.bass_utils import run_bass_kernel_spmd

    a = {k.replace("L0_", ""): np.asarray(v) for k, v in inputs.items()}
    lay = np.ascontiguousarray

    def by_pair(w):
        return lay(w.reshape(2, PAIRS, w.shape[1], w.shape[2]).transpose(0, 2, 1, 3).reshape(2 * w.shape[1], PAIRS, -1))

    up = np.stack([np.concatenate([a["ffn_Ws1"][None], a["ffn_W1"]]), np.concatenate([a["ffn_Wsg"][None], a["ffn_Wg"]])], 1)
    down = np.concatenate([a["ffn_Ws2"][None], a["ffn_W2"]])
    cos, sin = rotary_tables()
    arrays = {
        "x": a["x"].reshape(TOK, DM),
        "ctx": a["ctx_512"],
        "wqr": by_pair(a["xattn_W_qr"].transpose(0, 2, 1)),
        "wkr": by_pair(a["xattn_W_kr"].transpose(0, 2, 1)),
        "kcq": lay(a["xattn_w_kc_q"].reshape(HEADS, DK, 2, 96).transpose(3, 0, 2, 1)),
        "wq": a["xattn_Wq"],
        "kckv": lay(a["xattn_w_kc_kv"].transpose(1, 0, 2)),
        "wo": lay(a["xattn_Wo"].reshape(DM, HEADS, DK).transpose(2, 1, 0)),
        "w_up": lay(up.reshape(EXPERTS, 2, 2, 128, HID).transpose(3, 0, 1, 2, 4)),
        "w_down": lay(down.reshape(EXPERTS, 2, 128, DM).transpose(2, 0, 1, 3)),
        "gate_w": lay(a["ffn_gate_w"].reshape(2, 128, ROUTED).transpose(1, 0, 2)),
        "gate_b": lay(np.broadcast_to(a["ffn_gate_b"], (TP, 2, ROUTED))),
        "biases": lay(np.broadcast_to(a["ffn_biases"], (TP, 2, ROUTED))),
        "before": lay(np.broadcast_to(np.tril(np.ones((ROUTED, ROUTED), np.float32), -1), (TP, 2, ROUTED, ROUTED))),
        "cos": cos,
        "sin": sin,
    }
    nc = bacc.Bacc("TRN2", target_bir_lowering=False, num_devices=1)
    args = [nc.dram_tensor(f"in_{n}", v.shape, mybir.dt.from_np(v.dtype), kind="ExternalInput").ap() for n, v in arrays.items()]
    out = nc.dram_tensor("out", (TOK, DM), F32, kind="ExternalOutput").ap()
    build(nc, *args, out)
    r = run_bass_kernel_spmd(nc, [{f"in_{n}": v for n, v in arrays.items()}], core_ids=[0])
    return r.results[0]["out"].reshape(BATCH, SEQ, DM)
```

```python
from contextlib import ExitStack

import numpy as np

import concourse.bass as bass
from concourse import mybir

F32 = mybir.dt.float32
F16 = mybir.dt.float16
ALU = mybir.AluOpType
ACT = mybir.ActivationFunctionType
X_AXIS = mybir.AxisListType.X

BATCH, SEQ, DM = 8, 56, 256
KEYS, DC = 1500, 64
HEADS, DK, DCQ, RANK = 16, 128, 192, 64
PAIRS = HEADS // 2
TOK = BATCH * SEQ
HALF = PAIRS * SEQ
ROWS = 2 * HALF
KP, KT_N = 125, 12
STEPS = 2 * KT_N
RT = ROWS // 128
MXQ = 3
MXC = KEYS // MXQ
CHUNKS = RT * MXQ
RING = 12
TT, TP = 4, 112
EXPERTS, ROUTED, TOP_K, HID = 8, 7, 3, 256
LN_EPS = 1e-5
TAIL_AFTER = 3
QS = 16.0
WS, HS = 64.0, 16.0
EW = 3 * 2 * HID
W_PARTS = 3
FIRST_ORDER = [0, 4, 1, 5, 2, 6, 3]

POOL_TILES = [0, 1, 2, 4, 6, 8, 10]
DVE_TILES = [t for t in range(KT_N) if t not in POOL_TILES]
POOL_ADDS, DVE_ADDS = 2 * (len(POOL_TILES) - 1), 2 * (len(DVE_TILES) - 1)


def max_chunks_at(k):
    return [c for c in range(CHUNKS) if 3 + c * 17 // CHUNKS == k]


def high_at(c):
    return (7, 9, 12) if c < 7 else (6, 8, 10)


def low_at(c):
    return (9, 21, 23) if c < 7 else (9, 12, 14)


def adds_after(tiles, t, j):
    i = max(tiles.index(t), 1)
    return 2 * (i - 1) + j + 1


def build(nc, x, ctx, wqr, wkr, kcq, wq, kckv, wo, w_exp, gate_w, gate_b, biases, before, cos, sin, out):
    es = ExitStack()
    with es:
        def sb(name, shape, dt=F32):
            return es.enter_context(nc.sbuf_tensor(name, shape, dt))

        def sem(name):
            return es.enter_context(nc.semaphore(name))

        Q_hi = sb("Q_hi", [128, BATCH * ROWS], F16)
        Q_lo = sb("Q_lo", [128, BATCH * ROWS], F16)
        K_both = [sb(f"K_both{i}", [128, KT_N, KP], F16) for i in range(2)]
        K_hi1 = [sb(f"K_hi1{i}", [128, KT_N, KP], F16) for i in range(2)]
        V = [sb(f"V{i}", [KP, KT_N, DC]) for i in range(2)]
        roped = sb("roped", [KP, KT_N, DC])
        rot = sb("rot", [KP, KT_N, DC])
        K_split = sb("K_split", [KP, KT_N, 2 * DC], F16)
        kv = sb("kv", [128, BATCH, KT_N * DC])
        cs = sb("cs", [KP, 2, KT_N * DC])
        W = sb("W", [128, 12288])
        Wq = W[:, 0:4096].rearrange("p (h d) -> p h d", h=HEADS)
        Kcq = W[0:96, 4096:8192].rearrange("p (h c k) -> p h c k", h=HEADS, c=2)
        stage_hi = W[:, 4096:5888].bitcast(F16)
        stage_lo = W[:, 5888:7680].bitcast(F16)
        WoT = W[:, 8192:12288].rearrange("p (h o) -> p h o", h=HEADS)
        W_hi = W[:, 0:6144].bitcast(F16).rearrange("p (e n) -> p e n", e=EXPERTS)
        W_lo = W[:, 6144:12288].bitcast(F16).rearrange("p (e n) -> p e n", e=EXPERTS)
        G = sb("G", [128, 11776])
        Wqr = G[:, 0:1536].rearrange("p (n q) -> p n q", n=PAIRS)
        Wkr = G[:, 1536:2560].rearrange("p (n c) -> p n c", n=PAIRS)
        Kckv = G[:, 2560:3584].rearrange("p (h c) -> p h c", h=HEADS)
        A1 = G[0:96, 3584:5632].rearrange("p (n c d) -> p n c d", n=PAIRS, c=2)
        A2T = G[:, 5632:6656].rearrange("p (n k) -> p n k", n=PAIRS)
        A2 = G[:, 6656:7680].rearrange("p (n c) -> p n c", n=PAIRS)
        A3T = G[:, 7680:9728].rearrange("p (n d) -> p n d", n=PAIRS)
        A3 = G[:, 9728:11776].rearrange("p (n c k) -> p n c k", n=PAIRS, c=2)
        stage_q = G[:, 3584:7168]
        raw_w = G[:, 8960:8960 + EW]
        xn1 = G[0:TP, 9728:10752].rearrange("p (i d) -> p i d", i=TT)
        Pr = G[0:KP, 0:RING * HALF].rearrange("p (s n) -> p s n", s=RING)
        o = RING * HALF
        acc_dve = [G[0:KP, o + i * ROWS:o + (i + 1) * ROWS].rearrange("p (j n) -> p j n", j=2) for i in range(2)]
        o += 2 * ROWS
        acc_pool = [G[0:KP, o + i * ROWS:o + (i + 1) * ROWS].rearrange("p (j n) -> p j n", j=2) for i in range(2)]
        ctx_raw = sb("ctx_raw", [128, HALF])
        sums = sb("sums", [128, HALF])
        sums_thin = sb("sums_thin", [128, 7])
        recip_thin = sb("recip_thin", [128, 7])
        recip_row = sb("recip_row", [2, HALF])
        recip = sb("recip", [128, HALF])
        ctxT = sb("ctxT", [128, PAIRS, TP])
        VF = sb("VF", [128, PAIRS, DM])
        x_sb = sb("x_sb", [TP, TT, DM])
        xnT = sb("xnT", [128, 2, TOK])
        stats = sb("stats", [TP, TT, 6])
        mv = sb("mv", [TP, TT, 2])
        std = sb("std", [TP, TT])
        rstd = sb("rstd", [TP, TT])
        mx_part = sb("mx_part", [128, RT, MXQ])
        mx = sb("mx", [128, RT])
        mx16 = sb("mx16", [128, RT], F16)
        ident = sb("ident", [128, 128])
        ident16 = sb("ident16", [128, 128], F16)
        ones = sb("ones", [128, DC])
        gw = sb("gw", [128, 2, ROUTED])
        gb = sb("gb", [TP, 2, ROUTED])
        bi = sb("bi", [TP, 2, ROUTED])
        bef = sb("bef", [TP, 2, ROUTED, ROUTED])
        kvf = kv[:, :, :].rearrange("p b n -> p (b n)")
        silu_sb = kvf[:, 0:448]
        h_sb = kvf[:, 448:896]
        h_hi, h_lo = ([kvf[:, 896 + 448 * i + 224 * k:1120 + 448 * i + 224 * k].bitcast(F16).rearrange("p (c n) -> p c n", c=2)
                       for i in range(2)] for k in range(2))
        W_hi_flat, W_lo_flat = (w.rearrange("p e n -> p (e n)") for w in (W_hi, W_lo))
        x_hi, x_lo = (kvf[:, 2000 + 448 * k:2448 + 448 * k].bitcast(F16).rearrange("p (c n) -> p c n", c=2) for k in range(2))
        xn2 = kvf[0:TP, 3000:4024].rearrange("p (i d) -> p i d", i=TT)
        gate = {name: kvf[0:TP, 4100 + 16 * i:4114 + 16 * i].rearrange("p (i e) -> p i e", i=2)
                for i, name in enumerate(("logit", "shifted", "exp", "prob", "biased", "rank", "picked"))}
        gate1 = {name: kvf[0:TP, 4300 + 4 * i:4302 + 4 * i] for i, name in enumerate(("max", "sum", "rsum", "wsum", "rwsum"))}
        weight = kvf[0:TP, 4400:4428].rearrange("p (i e) -> p i e", i=TT)
        above, equal = (kvf[0:TP, 4500 + 100 * i:4598 + 100 * i].rearrange("p (i e f) -> p i e f", i=2, e=ROUTED) for i in range(2))

        banks = [es.enter_context(nc.psum_tensor(f"bank{i}", [128, 512], F32)) for i in range(8)]
        MX, ST, PV, AUX = banks[0:2], banks[2:5], banks[5], banks[6:8]

        in_x, in_fold1, in_fold2, in_wq, in_vfold, in_kv0, in_kvs, in_cs, in_gate, in_experts = (
            sem("in_" + n) for n in ("x", "fold1", "fold2", "wq", "vfold", "kv0", "kvs", "cs", "gate", "experts"))
        consts_ready, clear_ready = sem("consts_ready"), sem("clear_ready")
        pool_seq, dve_seq = sem("pool_seq"), sem("dve_seq")
        var_ready, std_ready, xn_ready, xt_made, xt_act, xt_dve = (
            sem(n) for n in ("var_ready", "std_ready", "xn_ready", "xt_made", "xt_act", "xt_dve"))
        fold_made, fold_act, fold_dve, q_made, q0_hi_ready, q0_lo_ready, q_copied, q_staged, q_lo_staged, q_spread, vf_made, vf_ready = (
            sem(n) for n in ("fold_made", "fold_act", "fold_dve", "q_made", "q0_hi_ready", "q0_lo_ready", "q_copied", "q_staged",
                             "q_lo_staged", "q_spread", "vf_made", "vf_ready"))
        rope_ready, k_hi_ready, k_lo_ready, kt_made, kt_ready, k_hi1_copied, v_copied = (
            sem(n) for n in ("rope_ready", "k_hi_ready", "k_lo_ready", "kt_made", "kt_ready", "k_hi1_copied", "v_copied"))
        mx_made, mx_read, mx_whole, mx16_ready, m_made, m_ready = (
            sem(n) for n in ("mx_made", "mx_read", "mx_whole", "mx16_ready", "m_made", "m_ready"))
        st_made, exp_done, pv_done, ctx_saved, dve_added, pool_added = (
            sem(n) for n in ("st_made", "exp_done", "pv_done", "ctx_saved", "dve_added", "pool_added"))
        sum_merged, w_hi_ready, w_lo_ready, sum_made, sum_saved, sum_thin, recip_done, recip_rowed, recip_wide, ctx_ready, proj_made, x1_ready = (
            sem(n) for n in ("sum_merged", "w_hi_ready", "w_lo_ready", "sum_made", "sum_saved", "sum_thin", "recip_done", "recip_rowed", "recip_wide",
                             "ctx_ready", "proj_made", "x1_ready"))
        x_lo_ready, up_made, silu_done, h_made, h_hi_ready, h_lo_ready, down_made, y_ready, gate_made, logits_shifted, gexp_done, w_ready, sent = (
            sem(n) for n in ("x_lo_ready", "up_made", "silu_done", "h_made", "h_hi_ready", "h_lo_ready", "down_made", "y_ready", "gate_made", "logits_shifted", "gexp_done",
                             "w_ready", "sent"))

        block = es.enter_context(nc.Block())

        def batches(eng, body):
            body(0, 0)
            with eng.Fori(0, 2) as n:
                body(n, 1)
                body(n, 2)
            for b in (5, 6, 7):
                body(0, b)

        def first(n, c):
            return c == 0

        def has_next(n, c):
            return c < 7

        def has_rope(n, c):
            return c < 6

        @block.sync
        def _(sp):
            sp.dma_start(Wqr, wqr).then_inc(in_fold1, 16)
            sp.wait_ge(clear_ready, 1)
            for j in range(2):
                sp.dma_start(Wkr[64 * j:64 * j + 64, :, 64 * j:64 * j + 64], wkr[64 * j:64 * j + 64]).then_inc(in_fold1, 16)
            sp.dma_start(x_sb[:], x.rearrange("(i p) d -> p i d", p=TP)).then_inc(in_x, 16)
            sp.dma_start(Kcq, kcq).then_inc(in_fold2, 16)
            sp.dma_start(kv[0:KP, 0, :], ctx[0].rearrange("(p t) c -> p (t c)", p=KP)).then_inc(in_kv0, 16)
            sp.dma_start(cs[:, 0, :], cos).then_inc(in_cs, 16)
            sp.dma_start(cs[:, 1, :], sin).then_inc(in_cs, 16)
            sp.dma_start(Wq, wq.rearrange("(h k) d -> k h d", k=DK)).then_inc(in_wq, 16)
            sp.dma_start(Kckv, kckv).then_inc(in_vfold, 16)
            sp.dma_start(WoT, wo).then_inc(in_vfold, 16)
            for b in range(1, BATCH):
                sp.dma_start(kv[0:KP, b, :], ctx[b].rearrange("(p t) c -> p (t c)", p=KP)).then_inc(in_kvs, 16)
            sp.dma_start(gw[:], gate_w).then_inc(in_gate, 16)
            sp.dma_start(gb[:], gate_b).then_inc(in_gate, 16)
            sp.dma_start(bi[:], biases).then_inc(in_gate, 16)
            sp.dma_start(bef[:], before).then_inc(in_gate, 16)

            def copy_v(n, c):
                b = 2 * n + c
                sp.wait_ge(rope_ready, b + 1)
                if c >= 2:
                    sp.wait_ge(pv_done, KT_N * (b - 1))
                sp.dma_start(V[c % 2][:], roped[:]).then_inc(v_copied, 16)

            def copy_k(n, c):
                b = 2 * n + c
                sp.wait_ge(kt_ready, 2 * (b + 1))
                sp.dma_start(K_hi1[c % 2][0:64], K_both[c % 2][0:64]).then_inc(k_hi1_copied, 16)

            def load_expert(n, c):
                b = 2 * n + c
                if c >= 1:
                    sp.wait_ge(w_lo_ready, W_PARTS * b)
                sp.dma_start(raw_w, w_exp[bass.ds(b, 1)].rearrange("e p n -> (e p) n")).then_inc(in_experts, 16)

            copy_v(0, 0)
            copy_k(0, 0)
            Qh, Ql = (q[:, ROWS:].rearrange("p (b j n) -> p b j n", b=BATCH - 1, j=2) for q in (Q_hi, Q_lo))
            Sh, Sl = (q[:, HALF:].rearrange("p (b n) -> p b n", b=BATCH - 1) for q in (stage_hi, stage_lo))
            sp.wait_ge(q_staged, PAIRS)
            for j in range(2):
                for to in range(2):
                    sp.dma_start(Qh[64 * to:64 * to + 64, :, j], Sh[64 * j:64 * j + 64]).then_inc(q_spread, 16)
            sp.wait_ge(q_lo_staged, PAIRS)
            for j in range(2):
                sp.dma_start(Ql[0:64, :, j], Sl[64 * j:64 * j + 64]).then_inc(q_spread, 16)
            sp.wait_ge(q_spread, 6 * 16)
            sp.wait_ge(vf_ready, PAIRS)

            def normaliser(n, c):
                b = 2 * n + c
                sp.wait_ge(sum_saved, b + 1)
                for j in range(2):
                    sp.dma_start(sums_thin[64 * j:64 * j + 64, :], sums[64 * j:64 * j + 1, :]).then_inc(sum_thin, 16)
                sp.wait_ge(recip_done, b + 1)
                for j in range(2):
                    sp.dma_start(recip_row[j:j + 1, :], recip_thin[64 * j:64 * j + 64, :]).then_inc(recip_rowed, 16)
                sp.wait_ge(recip_rowed, 32 * (b + 1))
                for j in range(2):
                    sp.dma_start(recip[64 * j:64 * j + 64, :],
                                 recip_row[j:j + 1, :].unsqueeze(1).to_broadcast([1, 64, HALF])).then_inc(recip_wide, 16)

            def body(n, c):
                if has_next(n, c):
                    copy_v(n, c + 1)
                load_expert(n, c)
                if has_next(n, c):
                    copy_k(n, c + 1)
                if not first(n, c):
                    normaliser(n, c - 1)

            batches(sp, body)
            normaliser(0, 7)
            for g in range(2):
                sp.wait_ge(y_ready, 2 * EXPERTS * (g + 1))
                sp.dma_start(out.rearrange("(i p) d -> p i d", p=TP)[:, 2 * g:2 * g + 2], x_sb[:, 2 * g:2 * g + 2, :]).then_inc(sent, 16)
            sp.wait_ge(sent, 32)

        @block.gpsimd
        def _(pool):
            nc.gpsimd.memset(Wkr, 0.0).then_inc(clear_ready, 1)
            nc.gpsimd.memset(ident[:], 0.0)
            nc.gpsimd.memset(ident16[:], 0.0)
            nc.gpsimd.memset(ones[:], 1.0).then_inc(pool_seq, 1)
            pool.wait_ge(pool_seq, 1)
            for m in (ident, ident16):
                last = nc.gpsimd.affine_select(out=m[:], in_=m[:], compare_op=ALU.not_equal, fill=1.0, base=0,
                                               pattern=[[-1, 128]], channel_multiplier=1)
            last.then_inc(consts_ready, 1)
            pool.wait_ge(consts_ready, 1)
            for i in range(2):
                nc.gpsimd.memset(K_hi1[i][64:128], 0.0)
            nc.gpsimd.memset(Q_lo[64:128, :].bitcast(F32), 0.0).then_inc(clear_ready, 1)
            pool.wait_ge(clear_ready, 2)
            for i in range(2):
                last = nc.gpsimd.memset(K_hi1[i][64:65], -QS)
            last.then_inc(consts_ready, 1)
            pool.wait_ge(consts_ready, 2)

            def rope(n, c):
                b = 2 * n + c
                raw = kvf[0:KP, bass.ds(b * (KT_N * DC), KT_N * DC)].rearrange("p (t c) -> p t c", c=DC)
                cosv, sinv = (cs[:, i, :].rearrange("p (t c) -> p t c", c=DC) for i in range(2))
                if c >= 1:
                    pool.wait_ge(v_copied, 16 * b)
                    pool.wait_ge(k_lo_ready, b)
                nc.gpsimd.tensor_tensor(roped[:], raw, cosv, ALU.mult)
                h = DC // 2
                nc.gpsimd.tensor_tensor(rot[:, :, 0:h], raw[:, :, h:DC], sinv[:, :, 0:h], ALU.mult)
                nc.gpsimd.tensor_tensor(rot[:, :, h:DC], raw[:, :, 0:h], sinv[:, :, h:DC], ALU.mult).then_inc(pool_seq, 1)
                pool.wait_ge(pool_seq, 2 + b)
                nc.gpsimd.tensor_tensor(roped[:], roped[:], rot[:], ALU.add).then_inc(rope_ready, 1)

            def low(n, c):
                b = 2 * n + c
                pool.wait_ge(k_hi_ready, b + 1)
                nc.gpsimd.tensor_tensor(K_split[:, :, DC:2 * DC], roped[:], K_split[:, :, 0:DC], ALU.subtract)\
                    .then_inc(k_lo_ready, 1)

            def add(n, c, i, j):
                b = 2 * n + c
                t = POOL_TILES[i]
                pool.wait_ge(exp_done, STEPS * b + 2 * t + j + 1)
                to = acc_pool[c % 2][:, j, :]
                if i == 1:
                    a = Pr[:, (2 * POOL_TILES[0] + j) % RING, :]
                else:
                    a = to
                    pool.wait_ge(pool_added, POOL_ADDS * b + 2 * (i - 1) + j - 1)
                nc.gpsimd.tensor_tensor(to, a, Pr[:, (2 * t + j) % RING, :], ALU.add).then_inc(pool_added, 1)

            pool.wait_ge(in_cs, 32)
            pool.wait_ge(in_kv0, 16)
            rope(0, 0)
            low(0, 0)
            pool.wait_ge(in_kvs, 16 * (BATCH - 1))
            rope(0, 1)
            for p in range(PAIRS):
                pool.wait_ge(q_staged, p + 1)
                part = slice(SEQ * p, SEQ * p + SEQ)
                hi, lo, q = (v.rearrange("q (b n) -> q b n", b=BATCH)[:, 1:, part] for v in (stage_hi, stage_lo, stage_q))
                nc.gpsimd.tensor_tensor(lo, q, hi, ALU.subtract).then_inc(q_lo_staged, 1)
            low(0, 1)

            def body(n, c):
                for j in range(2):
                    add(n, c, 1, j)
                if has_rope(n, c):
                    rope(n, c + 2)
                for i in range(2, len(POOL_TILES)):
                    if i == len(POOL_TILES) - 1 and has_rope(n, c):
                        low(n, c + 2)
                    for j in range(2):
                        add(n, c, i, j)

            batches(pool, body)


        @block.scalar
        def _(act):
            def copy(to, of, **k):
                return nc.scalar.activation(to, of, ACT.Copy, **k)

            def k_hi(n, c):
                b = 2 * n + c
                act.wait_ge(rope_ready, b + 1)
                if c >= 1:
                    act.wait_ge(kt_made, 2 * b)
                copy(K_split[:, :, 0:DC], roped[:]).then_inc(k_hi_ready, 1)

            def kt(n, c, i):
                b = 2 * n + c
                act.wait_ge(kt_made, 2 * b + i + 1)
                of = AUX[i][:, :].bitcast(F16).rearrange("p (t k) -> p t k", k=128)[:, 0:6, 0:KP]
                copy(K_both[c % 2][:, 6 * i:6 * i + 6, :], of).then_inc(kt_ready, 1)

            def m_row(n, c, j):
                b = 2 * n + c
                act.wait_ge(m_made, 2 * b + j + 1)
                copy(Q_lo[64:65, bass.ds(b * ROWS + j * HALF, HALF)], AUX[j][64:65, 0:HALF]).then_inc(m_ready, 1)

            def w_high(n, c, i):
                b = 2 * n + c
                act.wait_ge(in_experts, 16 * (b + 1))
                part = EW // W_PARTS
                copy(W_hi_flat[:, bass.ds(b * EW + i * part, part)], raw_w[:, i * part:(i + 1) * part], scale=WS)\
                    .then_inc(w_hi_ready, 1)

            def save_ctx(n, c):
                b = 2 * n + c
                act.wait_ge(pv_done, KT_N * (b + 1))
                if c >= 1:
                    act.wait_ge(ctx_ready, b)
                copy(ctx_raw[:], PV[:, 0:HALF]).then_inc(ctx_saved, 1)

            def save_sums(n, c):
                b = 2 * n + c
                act.wait_ge(sum_made, b + 1)
                if c >= 1:
                    act.wait_ge(sum_thin, 32 * b)
                copy(sums[:], AUX[0][:, 0:HALF]).then_inc(sum_saved, 1)

            def norm(g):
                act.wait_ge(var_ready, g + 2)
                nc.scalar.activation(std[:, 2 * g:2 * g + 2], rstd[:, 2 * g:2 * g + 2], ACT.Sqrt).then_inc(std_ready, 1)

            def spread_x(g):
                act.wait_ge(xt_made, TT + g + 1)
                for to in (x_hi, xnT):
                    for i in range(2):
                        last = copy(to[:, :, TP * (2 * g + i):TP * (2 * g + i + 1)],
                                    banks[6][:, 2 * TP * i:2 * TP * (i + 1)].rearrange("p (c n) -> p c n", c=2))
                last.then_inc(xt_act, 1)

            def gate_exp(g):
                act.wait_ge(logits_shifted, g + 1)
                nc.scalar.activation(gate["exp"], gate["shifted"], ACT.Exp).then_inc(gexp_done, 1)

            fold_to = [lambda p: (A1[:, p], banks[p][0:96, 0:256]), lambda p: (A2T[:, p], banks[p][:, 0:128]),
                       lambda p: (A2[:, p], banks[p][:, 0:128]), lambda p: (A3T[:, p], banks[p][:, 0:256]),
                       lambda p: (A3[:, p], banks[p][:, 0:256])]
            for s in range(5):
                for p in range(0, PAIRS, 2):
                    act.wait_ge(fold_made, PAIRS * s + p + 1)
                    to, of = fold_to[s](p)
                    if len(to.shape) == 3:
                        of = of.rearrange("p (c n) -> p c n", c=2)
                    copy(to, of).then_inc(fold_act, 1)
                if s == 0:
                    act.wait_ge(var_ready, 1)
                    nc.scalar.activation(std[:], rstd[:], ACT.Sqrt).then_inc(std_ready, 1)
                    nc.scalar.preload_act_table(ACT.Exp)
                if s == 3:
                    k_hi(0, 0)
                if s == 4:
                    for i in range(2):
                        kt(0, 0, i)
                if s == 2:
                    for i in (0, 2):
                        act.wait_ge(xt_made, i + 1)
                        copy(xnT[:, :, TP * i:TP * i + TP], banks[i][:, 0:2 * TP].rearrange("p (c n) -> p c n", c=2))\
                            .then_inc(xt_act, 1)
            for p in range(PAIRS):
                act.wait_ge(q_made, p + 1)
                of = banks[2 + p % 6]
                for j in range(2):
                    for to in range(2):
                        last = copy(Q_hi[64 * to:64 * to + 64, HALF * j + SEQ * p:HALF * j + SEQ * p + SEQ],
                                    of[64 * j:64 * j + 64, 0:SEQ], scale=QS)
                last.then_inc(q0_hi_ready, 1)
                q, hi = (v.rearrange("q (b n) -> q b n", b=BATCH)[:, :, SEQ * p:SEQ * p + SEQ] for v in (stage_q, stage_hi))
                of = of[:, 0:TOK].rearrange("q (b s) -> q b s", b=BATCH)
                copy(q, of, scale=QS).then_inc(q_copied, 1)
                copy(hi[:, 1:], of[:, 1:], scale=QS).then_inc(q_staged, 1)
            k_hi(0, 1)
            for p in range(PAIRS):
                act.wait_ge(vf_made, p + 1)
                copy(VF[:, p], banks[2 + p % 4][:, 0:DM]).then_inc(vf_ready, 1)
            for j in range(2):
                m_row(0, 0, j)

            def body(n, c):
                b = 2 * n + c
                for k in range(STEPS):
                    act.wait_ge(st_made, STEPS * b + k + 1)
                    if not (first(n, c) and k < RING):
                        bb, kk = (b, k - RING) if k >= RING else (b - 1, k - RING + STEPS)
                        act.wait_ge(pv_done, KT_N * bb + kk // 2 + 1)
                        t, j = kk // 2, kk % 2
                        if t in POOL_TILES:
                            act.wait_ge(pool_added, POOL_ADDS * bb + adds_after(POOL_TILES, t, j))
                        else:
                            act.wait_ge(dve_added, DVE_ADDS * bb + adds_after(DVE_TILES, t, j))
                    nc.scalar.activation(Pr[:, k % RING, :], ST[k % 3][0:KP, 0:HALF], ACT.Exp, scale=1.0 / QS)\
                        .then_inc(exp_done, 1)
                    if k < 2 and has_next(n, c):
                        kt(n, c + 1, k)
                    if k == 2 and not first(n, c):
                        save_ctx(n, c - 1)
                    if k == 7 and not first(n, c):
                        save_sums(n, c - 1)
                    if k in high_at(c):
                        w_high(n, c, high_at(c).index(k))
                    if k == 13 and has_rope(n, c):
                        k_hi(n, c + 2)
                    if k in (21, 22) and has_next(n, c):
                        m_row(n, c + 1, k - 21)
                    if c == 7:
                        if k == 9:
                            norm(0)
                        if k == 14:
                            spread_x(0)
                        if k == 18:
                            gate_exp(0)

            batches(act, body)
            save_ctx(0, 7)
            for u in range(2 * EXPERTS):
                act.wait_ge(up_made, u + 1)
                if u >= 1:
                    act.wait_ge(h_made, u)
                nc.scalar.activation(silu_sb, banks[2 * (u % 2)][:, 0:4 * TP], ACT.Silu, scale=1.0 / WS).then_inc(silu_done, 1)
                act.wait_ge(h_made, u + 1)
                if u >= 2:
                    act.wait_ge(down_made, u - 1)
                copy(h_hi[u % 2].rearrange("p c n -> p (c n)"), h_sb).then_inc(h_hi_ready, 1)
                if u == 0:
                    save_sums(0, 7)
                if u == TAIL_AFTER:
                    norm(1)
                if u == EXPERTS - 2:
                    spread_x(1)
                    gate_exp(1)

        @block.vector
        def _(dve):
            chain = [0]

            def link(ins):
                chain[0] += 1
                ins.then_inc(dve_seq, 1)
                dve.wait_ge(dve_seq, chain[0])

            def norm(tiles):
                lo, hi = tiles[0], tiles[-1] + 1
                for i in tiles:
                    last = nc.vector.bn_stats(stats[:, i, :], x_sb[:, i, :])
                link(last)
                for i in tiles:
                    last = nc.vector.bn_aggr(mv[:, i, :], stats[:, i, :])
                link(last)
                nc.vector.tensor_scalar(rstd[:, lo:hi], mv[:, lo:hi, 1], LN_EPS, None, ALU.add).then_inc(var_ready, 1)

            def normalise(tiles, k, xn):
                lo, hi = tiles[0], tiles[-1] + 1
                dve.wait_ge(std_ready, k + 1)
                link(nc.vector.reciprocal(rstd[:, lo:hi], std[:, lo:hi]))
                for i in tiles:
                    last = nc.vector.tensor_scalar(xn[:, i, :], x_sb[:, i, :], mv[:, i, 0:1], rstd[:, i:i + 1],
                                                   ALU.subtract, ALU.mult)
                last.then_inc(xn_ready, 1)

            fold_to = [lambda p: (A1[:, p], banks[p][0:96, 0:256]), lambda p: (A2T[:, p], banks[p][:, 0:128]),
                       lambda p: (A2[:, p], banks[p][:, 0:128]), lambda p: (A3T[:, p], banks[p][:, 0:256]),
                       lambda p: (A3[:, p], banks[p][:, 0:256])]
            for s in range(5):
                for p in range(1, PAIRS, 2):
                    dve.wait_ge(fold_made, PAIRS * s + p + 1)
                    to, of = fold_to[s](p)
                    if len(to.shape) == 3:
                        of = of.rearrange("p (c n) -> p c n", c=2)
                    nc.vector.tensor_copy(to, of).then_inc(fold_dve, 1)
                if s == 0:
                    dve.wait_ge(in_x, 16)
                    norm(range(TT))
                if s == 1:
                    normalise(range(TT), 0, xn1)
                if s == 2:
                    for i in (1, 3):
                        dve.wait_ge(xt_made, i + 1)
                        nc.vector.tensor_copy(xnT[:, :, TP * i:TP * i + TP],
                                              banks[i][:, 0:2 * TP].rearrange("p (c n) -> p c n", c=2)).then_inc(xt_dve, 1)
            def reduce_chunk(n, c, i, of=None):
                b = 2 * n + c
                dve.wait_ge(mx_made, CHUNKS * b + i + 1)
                r, q = divmod(i if of is None else of, MXQ)
                nc.vector.tensor_reduce(mx_part[:, r, q:q + 1], MX[(c + i) % 2][:, 0:MXC],
                                        X_AXIS, ALU.max).then_inc(mx_read, 1)

            def maxima(n, c):
                b = 2 * n + c
                dve.wait_ge(mx_read, CHUNKS * (b + 1))
                nc.vector.tensor_reduce(mx[:], mx_part[:], X_AXIS, ALU.max).then_inc(mx_whole, 1)
                dve.wait_ge(mx_whole, b + 1)
                nc.vector.tensor_scalar(mx16[:], mx[:], 1.0 / QS, None, ALU.mult).then_inc(mx16_ready, 1)

            def add(n, c, t, j):
                b = 2 * n + c
                i = DVE_TILES.index(t)
                if i == 0:
                    return
                dve.wait_ge(exp_done, STEPS * b + 2 * t + j + 1)
                to = acc_dve[c % 2][:, j, :]
                if i == 1:
                    a = Pr[:, (2 * DVE_TILES[0] + j) % RING, :]
                else:
                    a = to
                    dve.wait_ge(dve_added, DVE_ADDS * b + 2 * (i - 1) + j - 1)
                nc.vector.tensor_tensor(to, a, Pr[:, (2 * t + j) % RING, :], ALU.add).then_inc(dve_added, 1)

            def merge(n, c):
                b = 2 * n + c
                dve.wait_ge(pool_added, POOL_ADDS * (b + 1))
                dve.wait_ge(dve_added, DVE_ADDS * (b + 1))
                nc.vector.tensor_tensor(acc_dve[c % 2], acc_dve[c % 2], acc_pool[c % 2], ALU.add).then_inc(sum_merged, 1)

            def w_low(n, c, i):
                b = 2 * n + c
                dve.wait_ge(w_hi_ready, W_PARTS * b + i + 1)
                part = EW // W_PARTS
                at = bass.ds(b * EW + i * part, part)
                nc.vector.scalar_tensor_tensor(W_lo_flat[:, at], raw_w[:, i * part:(i + 1) * part], WS, W_hi_flat[:, at],
                                               ALU.mult, ALU.subtract).then_inc(w_lo_ready, 1)

            def reciprocals(n, c):
                b = 2 * n + c
                dve.wait_ge(sum_thin, 32 * (b + 1))
                nc.vector.reciprocal(recip_thin[:], sums_thin[:]).then_inc(recip_done, 1)

            def context(n, c):
                b = 2 * n + c
                dve.wait_ge(recip_wide, 32 * (b + 1))
                dve.wait_ge(ctx_saved, b + 1)
                at = SEQ * (c % 2)
                nc.vector.tensor_tensor(ctxT[:, :, at:at + SEQ], ctx_raw[:].rearrange("p (h s) -> p h s", h=PAIRS),
                                        recip[:].rearrange("p (h s) -> p h s", h=PAIRS), ALU.mult).then_inc(ctx_ready, 1)

            def residual(tile):
                dve.wait_ge(proj_made, tile + 1)
                at = x_flat[:, bass.ds(tile * DM, DM)]
                nc.vector.tensor_tensor(at, AUX[1][0:TP, 0:DM], at, ALU.add).then_inc(x1_ready, 1)

            def first_rows(i):
                for q in range(MXQ):
                    reduce_chunk(0, 0, MXQ * i + q, MXQ * FIRST_ORDER[i] + q)

            x_flat = x_sb[:, :, :].rearrange("p i d -> p (i d)")
            for p in range(PAIRS):
                if p >= 3:
                    first_rows(p - 3)
                dve.wait_ge(q0_hi_ready, p + 1)
                dve.wait_ge(q_copied, p + 1)
                for j in range(2):
                    part = slice(HALF * j + SEQ * p, HALF * j + SEQ * p + SEQ)
                    last = nc.vector.tensor_tensor(Q_lo[0:64, part], stage_q[64 * j:64 * j + 64, SEQ * p:SEQ * p + SEQ],
                                                   Q_hi[64 * j:64 * j + 64, part], ALU.subtract)
                last.then_inc(q0_lo_ready, 1)
            first_rows(5)
            first_rows(6)
            maxima(0, 0)

            def gating(g):
                dve.wait_ge(gate_made, g + 1)
                logit = banks[7][0:TP, 0:32].rearrange("p (i e) -> p i e", i=2)[:, :, 0:ROUTED]
                wide = lambda v: v.unsqueeze(2).to_broadcast([TP, 2, ROUTED])
                link(nc.vector.tensor_tensor(gate["logit"], logit, gb[:], ALU.add))
                link(nc.vector.tensor_reduce(gate1["max"], gate["logit"], X_AXIS, ALU.max))
                nc.vector.tensor_tensor(gate["shifted"], gate["logit"], wide(gate1["max"]), ALU.subtract).then_inc(logits_shifted, 1)
                dve.wait_ge(gexp_done, g + 1)
                link(nc.vector.tensor_reduce(gate1["sum"], gate["exp"], X_AXIS, ALU.add))
                link(nc.vector.reciprocal(gate1["rsum"], gate1["sum"]))
                link(nc.vector.tensor_tensor(gate["prob"], gate["exp"], wide(gate1["rsum"]), ALU.mult))
                link(nc.vector.tensor_tensor(gate["biased"], gate["prob"], bi[:], ALU.add))
                other = gate["biased"].unsqueeze(2).to_broadcast([TP, 2, ROUTED, ROUTED])
                own = gate["biased"].unsqueeze(3).to_broadcast([TP, 2, ROUTED, ROUTED])
                nc.vector.tensor_tensor(above, other, own, ALU.is_gt)
                link(nc.vector.tensor_tensor(equal, other, own, ALU.is_equal))
                link(nc.vector.tensor_tensor(equal, equal, bef[:], ALU.mult))
                link(nc.vector.tensor_tensor(above, above, equal, ALU.add))
                link(nc.vector.tensor_reduce(gate["rank"], above, X_AXIS, ALU.add))
                link(nc.vector.tensor_scalar(gate["rank"], gate["rank"], TOP_K - 0.5, None, ALU.is_lt))
                link(nc.vector.tensor_tensor(gate["picked"], gate["prob"], gate["rank"], ALU.mult))
                link(nc.vector.tensor_reduce(gate1["wsum"], gate["picked"], X_AXIS, ALU.add))
                link(nc.vector.reciprocal(gate1["rwsum"], gate1["wsum"]))
                link(nc.vector.tensor_scalar(gate1["rwsum"], gate1["rwsum"], 1.0 / (WS * HS), None, ALU.mult))
                link(nc.vector.tensor_tensor(weight[:, 2 * g:2 * g + 2], gate["picked"], wide(gate1["rwsum"]), ALU.mult))

            def x_low(g):
                dve.wait_ge(xt_act, 2 + g + 1)
                for i in range(2):
                    part = slice(TP * (2 * g + i), TP * (2 * g + i + 1))
                    last = nc.vector.tensor_tensor(x_lo[:, :, part],
                                                   banks[6][:, 2 * TP * i:2 * TP * (i + 1)].rearrange("p (c n) -> p c n", c=2),
                                                   x_hi[:, :, part], ALU.subtract)
                last.then_inc(x_lo_ready, 1)

            def combine(u):
                g, e = divmod(u, EXPERTS)
                dve.wait_ge(down_made, u + 1)
                for i in range(2):
                    t = 2 * g + i
                    of = banks[4 + u % 2][0:TP, DM * i:DM * i + DM]
                    if e == 0:
                        nc.vector.scalar_tensor_tensor(x_sb[:, t, :], of, 1.0 / (WS * HS), x_sb[:, t, :],
                                                       ALU.mult, ALU.add).then_inc(y_ready, 1)
                    else:
                        dve.wait_ge(y_ready, 2 * (u - 1) + i + 1)
                        nc.vector.scalar_tensor_tensor(x_sb[:, t, :], of, weight[:, t, e - 1:e], x_sb[:, t, :],
                                                       ALU.mult, ALU.add).then_inc(y_ready, 1)

            def body(n, c):
                for k in range(STEPS + 2):
                    if has_next(n, c):
                        for i in max_chunks_at(k):
                            reduce_chunk(n, c + 1, i)
                    if k >= 2 and (k - 2) // 2 in DVE_TILES:
                        add(n, c, (k - 2) // 2, k % 2)
                    if k == 10 and not first(n, c):
                        reciprocals(n, c - 1)
                    if k in low_at(c):
                        w_low(n, c, low_at(c).index(k))
                    if k == 15 and not first(n, c):
                        context(n, c - 1)
                    if k == 18 and c % 2 == 0 and not first(n, c):
                        residual(n + c // 2 - 1)
                    if k == 19 and has_next(n, c):
                        maxima(n, c + 1)
                    if c == 7:
                        if k == 6:
                            dve.wait_ge(x1_ready, 2)
                            norm((0, 1))
                        if k == 11:
                            normalise((0, 1), 1, xn2)
                        if k == 16:
                            x_low(0)
                        if k == 20:
                            gating(0)
                merge(n, c)


            batches(dve, body)
            for u in range(2 * EXPERTS):
                dve.wait_ge(silu_done, u + 1)
                if u >= 1:
                    dve.wait_ge(h_hi_ready, u)
                    dve.wait_ge(h_lo_ready, u)
                nc.vector.scalar_tensor_tensor(h_sb, banks[2 * (u % 2) + 1][:, 0:4 * TP], HS / WS, silu_sb,
                                               ALU.mult, ALU.mult).then_inc(h_made, 1)
                dve.wait_ge(h_hi_ready, u + 1)
                nc.vector.tensor_tensor(h_lo[u % 2].rearrange("p c n -> p (c n)"), h_sb,
                                        h_hi[u % 2].rearrange("p c n -> p (c n)"), ALU.subtract).then_inc(h_lo_ready, 1)
                if u >= 1:
                    combine(u - 1)
                if u == 1:
                    reciprocals(0, 7)
                if u == TAIL_AFTER - 1:
                    context(0, 7)
                if u == TAIL_AFTER:
                    residual(TT - 1)
                    dve.wait_ge(x1_ready, TT)
                    norm((2, 3))
                if u == TAIL_AFTER + 1:
                    normalise((2, 3), 2, xn2)
                if u == EXPERTS - 2:
                    x_low(1)
                    gating(1)
            combine(2 * EXPERTS - 1)

        @block.tensor
        def _(pe):
            def folded(s, p):
                pe.wait_ge(fold_act if p % 2 == 0 else fold_dve, 4 * s + p // 2 + 1)

            pe.wait_ge(consts_ready, 1)
            pe.wait_ge(in_fold1, 48)
            for p in range(PAIRS):
                for c in range(2):
                    last = nc.tensor.matmul(banks[p][0:96, 128 * c:128 * c + 128], Wqr[:, p, 96 * c:96 * c + 96],
                                            Wkr[:, p, :], start=True, stop=True)
                last.then_inc(fold_made, 1)
            pe.wait_ge(in_fold2, 16)
            for p in range(PAIRS):
                folded(0, p)
                for c in range(2):
                    for j in range(2):
                        last = nc.tensor.matmul(banks[p][64 * j:64 * j + 64, 0:128], A1[:, p, c, 64 * j:64 * j + 64],
                                                Kcq[:, p + PAIRS * j, c, :], start=(c == 0), stop=(c == 1))
                last.then_inc(fold_made, 1)
            for p in range(PAIRS):
                folded(1, p)
                nc.tensor.transpose(banks[p][:, 0:128], A2T[:, p, :], ident[:]).then_inc(fold_made, 1)
            pe.wait_ge(xn_ready, 1)
            for i in range(TT):
                folded(2, i)
                for c in range(2):
                    last = nc.tensor.transpose(banks[i][:, TP * c:TP * c + TP], xn1[:, i, 128 * c:128 * c + 128],
                                               ident[0:TP, 0:TP])
                last.then_inc(xt_made, 1)
            pe.wait_ge(in_wq, 16)
            for p in range(PAIRS):
                folded(2, p)
                if p < TT:
                    pe.wait_ge(xt_act if p % 2 == 0 else xt_dve, p // 2 + 1)
                for j in range(2):
                    last = nc.tensor.matmul(banks[p][64 * j:64 * j + 64, 0:DM], A2[:, p, 64 * j:64 * j + 64],
                                            Wq[:, p + PAIRS * j, :], start=True, stop=True)
                last.then_inc(fold_made, 1)
            for p in range(PAIRS):
                folded(3, p)
                for c in range(2):
                    last = nc.tensor.transpose(banks[p][:, 128 * c:128 * c + 128], A3T[:, p, 128 * c:128 * c + 128], ident[:])
                last.then_inc(fold_made, 1)
            def kt(n, c):
                b = 2 * n + c
                pe.wait_ge(k_lo_ready, b + 1)
                for t in range(KT_N):
                    to = AUX[t // 6][:, :].bitcast(F16)[:, 128 * (t % 6):128 * (t % 6) + KP]
                    last = nc.tensor.transpose(to, K_split[:, t, :], ident16[0:KP, 0:KP])
                    if t % 6 == 5:
                        last.then_inc(kt_made, 1)

            def max_chunk(n, c, i, of=None):
                b = 2 * n + c
                if i == 0:
                    pe.wait_ge(kt_ready, 2 * (b + 1))
                if not (c == 0 and i < 2):
                    pe.wait_ge(mx_read, CHUNKS * b + i - 1)
                r, q = divmod(i if of is None else of, MXQ)
                nc.tensor.matmul(MX[(c + i) % 2][:, 0:MXC], Q_hi[:, bass.ds(b * ROWS + 128 * r, 128)],
                                 K_both[c % 2][:, 4 * q:4 * q + 4, :].rearrange("p t k -> p (t k)"),
                                 start=True, stop=True).then_inc(mx_made, 1)

            def m_row(n, c):
                b = 2 * n + c
                pe.wait_ge(mx16_ready, b + 1)
                for j in range(2):
                    for r in range(RT):
                        lo, hi = max(128 * r, HALF * j), min(128 * r + 128, HALF * j + HALF)
                        if lo < hi:
                            last = nc.tensor.matmul(AUX[j][64:65, lo - HALF * j:hi - HALF * j], mx16[:, r:r + 1],
                                                    ident16[:, lo - 128 * r:hi - 128 * r], start=True, stop=True)
                    last.then_inc(m_made, 1)

            def pv(n, c, t):
                b = 2 * n + c
                pe.wait_ge(exp_done, STEPS * b + 2 * t + 2)
                if t == 0:
                    pe.wait_ge(v_copied, 16 * (b + 1))
                    if c >= 1:
                        pe.wait_ge(ctx_saved, b)
                for j in range(2):
                    last = nc.tensor.matmul(PV[64 * j:64 * j + 64, 0:HALF], V[c % 2][:, t, :], Pr[:, (2 * t + j) % RING, :],
                                            start=(t == 0), stop=(t == KT_N - 1))
                last.then_inc(pv_done, 1)

            def row_sums(n, c):
                b = 2 * n + c
                pe.wait_ge(sum_merged, b + 1)
                for j in range(2):
                    last = nc.tensor.matmul(AUX[0][64 * j:64 * j + 64, 0:HALF], ones[0:KP, :], acc_dve[c % 2][:, j, :],
                                            start=True, stop=True)
                last.then_inc(sum_made, 1)

            def project(n, c, parts):
                b = 2 * n + c
                if parts[0] == 0:
                    pe.wait_ge(ctx_ready, b + 1)
                for p in parts:
                    last = nc.tensor.matmul(AUX[1][0:TP, 0:DM], ctxT[:, p, :], VF[:, p, :], start=(p == 0), stop=(p == PAIRS - 1))
                if parts[-1] == PAIRS - 1:
                    last.then_inc(proj_made, 1)

            folded(4, 6)
            folded(4, 7)
            kt(0, 0)

            def first_rows(i, q):
                r = FIRST_ORDER[i]
                if q == 0:
                    heads = range(128 * r // SEQ, (128 * r + 127) // SEQ + 1)
                    pe.wait_ge(q0_hi_ready, max(h % PAIRS for h in heads) + 1)
                max_chunk(0, 0, MXQ * i + q, MXQ * r + q)

            for p in range(PAIRS):
                folded(4, p)
                if p in (4, 5):
                    pe.wait_ge(kt_ready, p - 3)
                if p >= 6:
                    pe.wait_ge(q_staged, p - 5)
                for c in range(2):
                    last = nc.tensor.matmul(banks[2 + p % 6][:, 0:TOK], A3[:, p, c, :], xnT[:, c, :],
                                            start=(c == 0), stop=(c == 1))
                    if p >= 3 and c == 0:
                        first_rows(p - 3, 0)
                last.then_inc(q_made, 1)
                if p >= 3:
                    first_rows(p - 3, 1)
                    first_rows(p - 3, 2)
            pe.wait_ge(in_vfold, 32)
            for p in range(PAIRS):
                if p < 4:
                    pe.wait_ge(q_staged, p + 1 + 6 * (p < 2))
                else:
                    pe.wait_ge(vf_ready, p - 3)
                for j in range(2):
                    last = nc.tensor.matmul(banks[2 + p % 4][64 * j:64 * j + 64, 0:DM], Kckv[:, p + PAIRS * j, :],
                                            WoT[:, p + PAIRS * j, :], start=True, stop=True)
                last.then_inc(vf_made, 1)
                if p >= 2:
                    first_rows(5 + (p - 2) // 3, (p - 2) % 3)
            pe.wait_ge(q_staged, 6)
            m_row(0, 0)
            pe.wait_ge(consts_ready, 2)
            pe.wait_ge(q0_lo_ready, PAIRS)
            pe.wait_ge(vf_ready, PAIRS)

            def transpose_x(g):
                pe.wait_ge(xn_ready, g + 2)
                for i in range(2):
                    for c in range(2):
                        last = nc.tensor.transpose(banks[6][:, TP * (2 * i + c):TP * (2 * i + c) + TP],
                                                   xn2[:, 2 * g + i, 128 * c:128 * c + 128], ident[0:TP, 0:TP])
                last.then_inc(xt_made, 1)

            def gate_logits(g):
                if g == 0:
                    pe.wait_ge(in_gate, 64)
                pe.wait_ge(xt_act, 2 + g + 1)
                pe.wait_ge(x1_ready, 3 + g)
                for i in range(2):
                    for c in range(2):
                        last = nc.tensor.matmul(banks[7][0:TP, 16 * i:16 * i + ROUTED],
                                                xnT[:, c, TP * (2 * g + i):TP * (2 * g + i + 1)], gw[:, c, :],
                                                start=(c == 0), stop=(c == 1))
                last.then_inc(gate_made, 1)

            def up(u):
                g, e = divmod(u, EXPERTS)
                if u >= 2:
                    pe.wait_ge(h_made, u - 1)
                at = slice(2 * TP * g, 2 * TP * (g + 1))
                for w in range(2):
                    for h in range(2):
                        terms = [(W, X, c) for c in range(2) for W, X in ((W_hi, x_hi), (W_hi, x_lo), (W_lo, x_hi))]
                        for n, (W, X, c) in enumerate(terms):
                            o = DM * (2 * w + c) + 128 * h
                            last = nc.tensor.matmul(banks[2 * (u % 2) + w][:, 2 * TP * h:2 * TP * (h + 1)],
                                                    W[:, e, o:o + 128], X[:, c, at], start=(n == 0), stop=(n == len(terms) - 1))
                last.then_inc(up_made, 1)

            def down(u):
                g, e = divmod(u, EXPERTS)
                pe.wait_ge(h_lo_ready, u + 1)
                if u >= 2:
                    pe.wait_ge(y_ready, 2 * (u - 1))
                for i in range(2):
                    terms = [(X, W, c) for c in range(2) for X, W in ((h_hi, W_hi), (h_hi, W_lo), (h_lo, W_hi))]
                    for n, (X, W, c) in enumerate(terms):
                        o = 4 * DM + DM * c
                        last = nc.tensor.matmul(banks[4 + u % 2][0:TP, DM * i:DM * i + DM], X[u % 2][:, c, TP * i:TP * i + TP],
                                                W[:, e, o:o + DM], start=(n == 0), stop=(n == len(terms) - 1))
                last.then_inc(down_made, 1)

            def body(n, c):
                b = 2 * n + c
                for k in range(STEPS):
                    t, j = divmod(k, 2)
                    rows = bass.ds(b * ROWS + HALF * j, HALF)
                    if k == 0:
                        pe.wait_ge(m_ready, 2 * (b + 1))
                        pe.wait_ge(k_hi1_copied, 16 * (b + 1))
                    if not (first(n, c) and k < 3):
                        pe.wait_ge(exp_done, STEPS * b + k - 2)
                    nc.tensor.matmul(ST[k % 3][0:KP, 0:HALF], K_both[c % 2][:, t, :], Q_hi[:, rows], start=True, stop=False)
                    nc.tensor.matmul(ST[k % 3][0:KP, 0:HALF], K_hi1[c % 2][:, t, :], Q_lo[:, rows], start=False, stop=True)\
                        .then_inc(st_made, 1)
                    if first(n, c) and k == 0:
                        pe.wait_ge(q_spread, 6 * 16)
                    if has_next(n, c):
                        if k == 0:
                            kt(n, c + 1)
                        for i in max_chunks_at(k)[:1]:
                            max_chunk(n, c + 1, i)
                    if k == 1 and not first(n, c):
                        pv(n, c - 1, KT_N - 1)
                    if j == 1 and t >= 1:
                        pv(n, c, t - 1)
                    if has_next(n, c):
                        for i in max_chunks_at(k)[1:]:
                            max_chunk(n, c + 1, i)
                    if k == 6 and not first(n, c):
                        if has_next(n, c):
                            pe.wait_ge(kt_ready, 2 * (b + 2))
                        row_sums(n, c - 1)
                    if k in (16, 17) and c % 2 == 0 and not first(n, c):
                        project(n, c - 1, range(4 * (k - 16), 4 * (k - 15)))
                    if c == 7 and k == 12:
                        pe.wait_ge(sum_saved, 7)
                        transpose_x(0)
                    if c == 7 and k == 17:
                        gate_logits(0)
                    if k == 21 and has_next(n, c):
                        if not first(n, c):
                            pe.wait_ge(sum_saved, b)
                        m_row(n, c + 1)

            batches(pe, body)
            pv(0, 7, KT_N - 1)
            pe.wait_ge(w_lo_ready, W_PARTS * EXPERTS)
            pe.wait_ge(x_lo_ready, 1)
            up(0)
            pe.wait_ge(x_lo_ready, 1)
            row_sums(0, 7)
            pe.wait_ge(ctx_saved, BATCH)
            for u in range(2 * EXPERTS):
                if u == TAIL_AFTER:
                    project(0, 7, range(PAIRS))
                if u == EXPERTS - 2:
                    transpose_x(1)
                    gate_logits(1)
                if u == EXPERTS - 1:
                    pe.wait_ge(x_lo_ready, 2)
                if u + 1 < 2 * EXPERTS:
                    up(u + 1)
                down(u)


def rotary_tables():
    inv_freq = np.float32(1.0) / np.float32(10000.0) ** (np.arange(0, DC, 2, dtype=np.float32) / np.float32(DC))
    angle = np.arange(KEYS, dtype=np.float32)[:, None] * inv_freq[None, :]
    sin, cos = (np.repeat(f(angle), 2, axis=-1).astype(np.float32) for f in (np.sin, np.cos))
    sin[:, :DC // 2] *= -1
    return [np.ascontiguousarray(a.reshape(KP, KT_N * DC)) for a in (cos, sin)]


def kernel(**inputs):
    import concourse.bacc as bacc
    from concourse.bass_utils import run_bass_kernel_spmd

    a = {k.replace("L0_", ""): np.asarray(v) for k, v in inputs.items()}
    lay = np.ascontiguousarray

    def by_pair(w):
        return lay(w.reshape(2, PAIRS, w.shape[1], w.shape[2]).transpose(0, 2, 1, 3).reshape(2 * w.shape[1], PAIRS, -1))

    up = np.stack([np.concatenate([a["ffn_Ws1"][None], a["ffn_W1"]]), np.concatenate([a["ffn_Wsg"][None], a["ffn_Wg"]])], 1)
    down = np.concatenate([a["ffn_Ws2"][None], a["ffn_W2"]])
    cos, sin = rotary_tables()
    arrays = {
        "x": a["x"].reshape(TOK, DM),
        "ctx": a["ctx_512"],
        "wqr": by_pair(a["xattn_W_qr"].transpose(0, 2, 1)),
        "wkr": by_pair(a["xattn_W_kr"].transpose(0, 2, 1)),
        "kcq": lay(a["xattn_w_kc_q"].reshape(HEADS, DK, 2, 96).transpose(3, 0, 2, 1)),
        "wq": a["xattn_Wq"],
        "kckv": lay(a["xattn_w_kc_kv"].transpose(1, 0, 2)),
        "wo": lay(a["xattn_Wo"].reshape(DM, HEADS, DK).transpose(2, 1, 0)),
        "w_exp": lay(np.concatenate([up.reshape(EXPERTS, 2, 2, 128, HID), down.reshape(EXPERTS, 1, 2, 128, DM)], 1)
                     .transpose(0, 3, 1, 2, 4).reshape(EXPERTS, 128, EW)),
        "gate_w": lay(a["ffn_gate_w"].reshape(2, 128, ROUTED).transpose(1, 0, 2)),
        "gate_b": lay(np.broadcast_to(a["ffn_gate_b"], (TP, 2, ROUTED))),
        "biases": lay(np.broadcast_to(a["ffn_biases"], (TP, 2, ROUTED))),
        "before": lay(np.broadcast_to(np.tril(np.ones((ROUTED, ROUTED), np.float32), -1), (TP, 2, ROUTED, ROUTED))),
        "cos": cos,
        "sin": sin,
    }
    nc = bacc.Bacc("TRN2", target_bir_lowering=False, num_devices=1)
    args = [nc.dram_tensor(f"in_{n}", v.shape, mybir.dt.from_np(v.dtype), kind="ExternalInput").ap() for n, v in arrays.items()]
    out = nc.dram_tensor("out", (TOK, DM), F32, kind="ExternalOutput").ap()
    build(nc, *args, out)
    r = run_bass_kernel_spmd(nc, [{f"in_{n}": v for n, v in arrays.items()}], core_ids=[0])
    return r.results[0]["out"].reshape(BATCH, SEQ, DM)
```

```python
from contextlib import ExitStack

import numpy as np

import concourse.bass as bass
from concourse import mybir

F32 = mybir.dt.float32
F16 = mybir.dt.float16
ALU = mybir.AluOpType
ACT = mybir.ActivationFunctionType
X_AXIS = mybir.AxisListType.X

BATCH, SEQ, DM = 8, 56, 256
KEYS, DC = 1500, 64
HEADS, DK, DCQ, RANK = 16, 128, 192, 64
PAIRS = HEADS // 2
TOK = BATCH * SEQ
HALF = PAIRS * SEQ
ROWS = 2 * HALF
KP, KT_N = 125, 12
STEPS = 2 * KT_N
RT = ROWS // 128
MXQ = 3
MXC = KEYS // MXQ
WARM_UP = 9
CHUNKS = RT * MXQ
RING = 12
TT, TP = 4, 112
EXPERTS, ROUTED, TOP_K, HID = 8, 7, 3, 256
LN_EPS = 1e-5
KT_AFTER = 1
NORM_AT = 16
TAIL_AT = 3
TWO_OUT = EXPERTS + 3
UPS = 3
QS = 16.0
WS, HS = 64.0, 16.0
EW = 3 * 2 * HID
W_PARTS = 3
FIRST_ORDER = [0, 4, 1, 5, 2, 6, 3]

POOL_TILES = [0, 1, 2, 4, 6, 8, 10]
DVE_TILES = [t for t in range(KT_N) if t not in POOL_TILES]
POOL_ADDS, DVE_ADDS = 2 * (len(POOL_TILES) - 1), 2 * (len(DVE_TILES) - 1)


def max_chunks_at(k):
    return [c for c in range(CHUNKS) if 3 + c * 17 // CHUNKS == k]


def high_at(c):
    return (10, 12, 14) if c == 0 else (7, 9, 12) if c < 7 else (6, 8, 10)


def low_at(c):
    return (13, 21, 23) if c == 0 else (9, 21, 23) if c < 7 else (9, 12, 14)


def adds_after(tiles, t, j):
    i = max(tiles.index(t), 1)
    return 2 * (i - 1) + j + 1


def build(nc, x, ctx, wqr, wkr, kcq, wq, kckv, wo, w_exp, gate_w, gate_b, biases, before, cos, sin, out):
    es = ExitStack()
    with es:
        def sb(name, shape, dt=F32):
            return es.enter_context(nc.sbuf_tensor(name, shape, dt))

        def sem(name):
            return es.enter_context(nc.semaphore(name))

        Q_hi = sb("Q_hi", [128, BATCH * ROWS], F16)
        Q_lo = sb("Q_lo", [128, BATCH * ROWS], F16)
        K_both = [sb(f"K_both{i}", [128, KT_N, KP], F16) for i in range(2)]
        K_hi1 = [sb(f"K_hi1{i}", [128, KT_N, KP], F16) for i in range(2)]
        V = [sb(f"V{i}", [KP, KT_N, DC]) for i in range(2)]
        roped = sb("roped", [KP, KT_N, DC])
        rot = sb("rot", [KP, KT_N, DC])
        K_split = sb("K_split", [KP, KT_N, 2 * DC], F16)
        kv = sb("kv", [128, BATCH, KT_N * DC])
        cs = sb("cs", [KP, 2, KT_N * DC])
        W = sb("W", [128, 12288])
        Wq = W[:, 0:4096].rearrange("p (h d) -> p h d", h=HEADS)
        Kcq = W[0:96, 4096:8192].rearrange("p (j n k) -> p j n k", j=2, n=PAIRS)
        stage_hi = W[:, 4096:5888].bitcast(F16)
        stage_lo = W[:, 5888:7680].bitcast(F16)
        WoT = W[:, 8192:12288].rearrange("p (h o) -> p h o", h=HEADS)
        W_hi = W[:, 0:6144].bitcast(F16).rearrange("p (e n) -> p e n", e=EXPERTS)
        W_lo = W[:, 6144:12288].bitcast(F16).rearrange("p (e n) -> p e n", e=EXPERTS)
        G = sb("G", [128, 11776])
        Wqr = G[:, 0:1536].rearrange("p (n q) -> p n q", n=PAIRS)
        Wkr = G[:, 1536:2560].rearrange("p (n c) -> p n c", n=PAIRS)
        Kckv = G[:, 2560:3584].rearrange("p (h c) -> p h c", h=HEADS)
        A1 = G[0:96, 3584:5632].rearrange("p (n c d) -> p n c d", n=PAIRS, c=2)
        A2T = G[:, 5632:6656].rearrange("p (n k) -> p n k", n=PAIRS)
        A2 = G[:, 6656:7680].rearrange("p (n c) -> p n c", n=PAIRS)
        A3T = G[:, 7680:9728].rearrange("p (n d) -> p n d", n=PAIRS)
        A3 = G[:, 9728:11776].rearrange("p (n c k) -> p n c k", n=PAIRS, c=2)
        stage_q = G[:, 3584:7168]
        raw_w = G[:, 8960:8960 + EW]
        xn1 = G[0:TP, 9728:10752].rearrange("p (i d) -> p i d", i=TT)
        Pr = G[0:KP, 0:RING * HALF].rearrange("p (s n) -> p s n", s=RING)
        o = RING * HALF
        acc_dve = [G[0:KP, o + i * ROWS:o + (i + 1) * ROWS].rearrange("p (j n) -> p j n", j=2) for i in range(2)]
        o += 2 * ROWS
        acc_pool = [G[0:KP, o + i * ROWS:o + (i + 1) * ROWS].rearrange("p (j n) -> p j n", j=2) for i in range(2)]
        ctx_raw = sb("ctx_raw", [128, HALF])
        sums = sb("sums", [128, HALF])
        sums_thin = sb("sums_thin", [128, 7])
        recip_thin = sb("recip_thin", [128, 7])
        recip_row = sb("recip_row", [2, HALF])
        recip = sb("recip", [128, HALF])
        ctxT = sb("ctxT", [128, PAIRS, TP])
        VF = sb("VF", [128, PAIRS, DM])
        x_sb = sb("x_sb", [TP, TT, DM])
        xnT = sb("xnT", [128, 2, TOK])
        stats = sb("stats", [TP, TT, 6])
        mv = sb("mv", [TP, TT, 2])
        std = sb("std", [TP, TT])
        rstd = sb("rstd", [TP, TT])
        mx_part = sb("mx_part", [128, RT, MXQ])
        mx = sb("mx", [128, RT])
        mx16 = sb("mx16", [128, RT], F16)
        ident = sb("ident", [128, 128])
        ident16 = sb("ident16", [128, 128], F16)
        ones = sb("ones", [128, DC])
        gw = sb("gw", [128, 2, ROUTED])
        gb = sb("gb", [TP, 2, ROUTED])
        bi = sb("bi", [TP, 2, ROUTED])
        bef = sb("bef", [TP, 2, ROUTED, ROUTED])
        kvf = kv[:, :, :].rearrange("p b n -> p (b n)")
        silu_sb = kvf[:, 0:448]
        h_sb = kvf[:, 448:896]
        h_hi, h_lo = ([kvf[:, 896 + 448 * i + 224 * k:1120 + 448 * i + 224 * k].bitcast(F16).rearrange("p (c n) -> p c n", c=2)
                       for i in range(2)] for k in range(2))
        W_hi_flat, W_lo_flat = (w.rearrange("p e n -> p (e n)") for w in (W_hi, W_lo))
        x_hi, x_lo = (kvf[:, 2000 + 448 * k:2448 + 448 * k].bitcast(F16).rearrange("p (c n) -> p c n", c=2) for k in range(2))
        xn2 = kvf[0:TP, 3000:4024].rearrange("p (i d) -> p i d", i=TT)
        gate = {name: kvf[0:TP, 4100 + 16 * i:4114 + 16 * i].rearrange("p (i e) -> p i e", i=2)
                for i, name in enumerate(("logit", "shifted", "exp", "prob", "biased", "rank", "picked"))}
        gate1 = {name: kvf[0:TP, 4300 + 4 * i:4302 + 4 * i] for i, name in enumerate(("max", "sum", "rsum", "wsum", "rwsum"))}
        weight = kvf[0:TP, 4400:4428].rearrange("p (i e) -> p i e", i=TT)
        above, equal = (kvf[0:TP, 4500 + 100 * i:4598 + 100 * i].rearrange("p (i e f) -> p i e f", i=2, e=ROUTED) for i in range(2))

        banks = [es.enter_context(nc.psum_tensor(f"bank{i}", [128, 512], F32)) for i in range(8)]
        MX, ST, PV, AUX = banks[0:2], banks[2:5], banks[5], banks[6:8]
        VF_BANKS = [banks[i] for i in (4, 5, 2, 3)]

        def out_bank(u):
            return AUX[u % 2] if u >= TWO_OUT else AUX[0]

        in_x, in_fold1, in_vfold, in_kv0, in_kv1, in_kvs, in_cs, in_gate, in_experts = (
            sem("in_" + n) for n in ("x", "fold1", "vfold", "kv0", "kv1", "kvs", "cs", "gate", "experts"))
        in_fold2, in_wq = ([sem(f"in_{n}_{half}") for half in ("first", "second")] for n in ("fold2", "wq"))
        consts_ready, clear_ready = sem("consts_ready"), sem("clear_ready")
        pool_seq, dve_seq = sem("pool_seq"), sem("dve_seq")
        var_ready, std_ready, xn_ready, xt_made, xt_act, xt_dve = (
            sem(n) for n in ("var_ready", "std_ready", "xn_ready", "xt_made", "xt_act", "xt_dve"))
        fold_made, fold_act, fold_dve, q_made, q0_hi_ready, q0_lo_ready, q_copied, q_staged, q_lo_staged, q1_spread, q_spread, vf_made, vf_ready = (
            sem(n) for n in ("fold_made", "fold_act", "fold_dve", "q_made", "q0_hi_ready", "q0_lo_ready", "q_copied", "q_staged",
                             "q_lo_staged", "q1_spread", "q_spread", "vf_made", "vf_ready"))
        rope_ready, k_hi_ready, k_lo_ready, kt_made, kt_ready, k_hi1_copied, v_copied = (
            sem(n) for n in ("rope_ready", "k_hi_ready", "k_lo_ready", "kt_made", "kt_ready", "k_hi1_copied", "v_copied"))
        mx_made, mx_read, mx_whole, mx16_ready, m_made, m_ready = (
            sem(n) for n in ("mx_made", "mx_read", "mx_whole", "mx16_ready", "m_made", "m_ready"))
        st_made, exp_done, pv_done, ctx_saved, dve_added, pool_added = (
            sem(n) for n in ("st_made", "exp_done", "pv_done", "ctx_saved", "dve_added", "pool_added"))
        sum_merged, w_hi_ready, w_lo_ready, sum_made, sum_saved, sum_thin, recip_done, recip_rowed, recip_wide, ctx_ready, proj_made, x1_ready = (
            sem(n) for n in ("sum_merged", "w_hi_ready", "w_lo_ready", "sum_made", "sum_saved", "sum_thin", "recip_done", "recip_rowed", "recip_wide",
                             "ctx_ready", "proj_made", "x1_ready"))
        x_lo_ready, up_made, silu_done, h_made, h_hi_ready, h_lo_ready, down_made, y_ready, gate_made, logits_shifted, gexp_done, w_ready, sent = (
            sem(n) for n in ("x_lo_ready", "up_made", "silu_done", "h_made", "h_hi_ready", "h_lo_ready", "down_made", "y_ready", "gate_made", "logits_shifted", "gexp_done",
                             "w_ready", "sent"))

        block = es.enter_context(nc.Block())

        def batches(eng, body):
            body(0, 0)
            with eng.Fori(0, 2) as n:
                body(n, 1)
                body(n, 2)
            for b in (5, 6, 7):
                body(0, b)

        def first(n, c):
            return c == 0

        def has_next(n, c):
            return c < 7

        def has_rope(n, c):
            return c < 6

        @block.sync
        def _(sp):
            sp.dma_start(Wqr, wqr).then_inc(in_fold1, 16)
            sp.wait_ge(clear_ready, 1)
            for j in range(2):
                sp.dma_start(Wkr[64 * j:64 * j + 64, :, 64 * j:64 * j + 64], wkr[64 * j:64 * j + 64]).then_inc(in_fold1, 16)
            for half, loaded in enumerate(in_fold2):
                sp.dma_start(Kcq[:, :, 4 * half:4 * half + 4], kcq[:, :, 4 * half:4 * half + 4]).then_inc(loaded, 16)
                if half == 0:
                    sp.dma_start(x_sb[:], x.rearrange("(i p) d -> p i d", p=TP)).then_inc(in_x, 16)
            for half, loaded in enumerate(in_wq):
                for j in range(2):
                    h = PAIRS * j + 4 * half
                    sp.dma_start(Wq[:, h:h + 4], wq[DK * h:DK * (h + 4)].rearrange("(h k) d -> k h d", k=DK)).then_inc(loaded, 16)
            sp.dma_start(kv[0:KP, 0, :], ctx[0].rearrange("(p t) c -> p (t c)", p=KP)).then_inc(in_kv0, 16)
            sp.dma_start(cs[:, 0, :], cos).then_inc(in_cs, 16)
            sp.dma_start(cs[:, 1, :], sin).then_inc(in_cs, 16)
            sp.dma_start(kv[0:KP, 1, :], ctx[1].rearrange("(p t) c -> p (t c)", p=KP)).then_inc(in_kv1, 16)
            sp.dma_start(Kckv, kckv).then_inc(in_vfold, 16)
            sp.dma_start(WoT, wo).then_inc(in_vfold, 16)
            def copy_v(n, c):
                b = 2 * n + c
                sp.wait_ge(rope_ready, b + 1)
                if c >= 2:
                    sp.wait_ge(pv_done, KT_N * (b - 1))
                sp.dma_start(V[c % 2][:], roped[:]).then_inc(v_copied, 16)

            copy_v(0, 0)
            for b in range(2, BATCH):
                sp.dma_start(kv[0:KP, b, :], ctx[b].rearrange("(p t) c -> p (t c)", p=KP)).then_inc(in_kvs, 16)
            sp.dma_start(gw[:], gate_w).then_inc(in_gate, 16)
            sp.dma_start(gb[:], gate_b).then_inc(in_gate, 16)
            sp.dma_start(bi[:], biases).then_inc(in_gate, 16)
            sp.dma_start(bef[:], before).then_inc(in_gate, 16)

            def copy_k(n, c):
                b = 2 * n + c
                sp.wait_ge(kt_ready, 2 * (b + 1))
                sp.dma_start(K_hi1[c % 2][0:64], K_both[c % 2][0:64]).then_inc(k_hi1_copied, 16)

            def load_expert(n, c):
                b = 2 * n + c
                if c >= 1:
                    sp.wait_ge(w_lo_ready, W_PARTS * b)
                sp.dma_start(raw_w, w_exp[bass.ds(b, 1)].rearrange("e p n -> (e p) n")).then_inc(in_experts, 16)

            copy_k(0, 0)
            copy_v(0, 1)
            Qh, Ql = (q[:, ROWS:].rearrange("p (b j n) -> p b j n", b=BATCH - 1, j=2) for q in (Q_hi, Q_lo))
            Sh, Sl = (q[:, HALF:].rearrange("p (b n) -> p b n", b=BATCH - 1) for q in (stage_hi, stage_lo))
            sp.wait_ge(q_staged, PAIRS)
            for of, spread in ((slice(0, 1), q1_spread), (slice(1, BATCH - 1), q_spread)):
                for j in range(2):
                    for to in range(2):
                        sp.dma_start(Qh[64 * to:64 * to + 64, of, j], Sh[64 * j:64 * j + 64, of]).then_inc(spread, 16)
            sp.wait_ge(q_lo_staged, PAIRS)
            for j in range(2):
                sp.dma_start(Ql[0:64, :, j], Sl[64 * j:64 * j + 64]).then_inc(q_spread, 16)
            sp.wait_ge(q1_spread, 4 * 16)
            sp.wait_ge(q_spread, 6 * 16)
            sp.wait_ge(vf_ready, PAIRS)

            def normaliser(n, c):
                b = 2 * n + c
                sp.wait_ge(sum_saved, b + 1)
                for j in range(2):
                    sp.dma_start(sums_thin[64 * j:64 * j + 64, :], sums[64 * j:64 * j + 1, :]).then_inc(sum_thin, 16)
                sp.wait_ge(recip_done, b + 1)
                for j in range(2):
                    sp.dma_start(recip_row[j:j + 1, :], recip_thin[64 * j:64 * j + 64, :]).then_inc(recip_rowed, 16)
                sp.wait_ge(recip_rowed, 32 * (b + 1))
                for j in range(2):
                    sp.dma_start(recip[64 * j:64 * j + 64, :],
                                 recip_row[j:j + 1, :].unsqueeze(1).to_broadcast([1, 64, HALF])).then_inc(recip_wide, 16)

            def body(n, c):
                if has_next(n, c) and not first(n, c):
                    copy_v(n, c + 1)
                load_expert(n, c)
                if has_next(n, c):
                    copy_k(n, c + 1)
                if not first(n, c):
                    normaliser(n, c - 1)

            batches(sp, body)
            normaliser(0, 7)
            for g, tiles in ((0, (0, 1)), (1, (2,)), (1, (3,))):
                sp.wait_ge(y_ready, 2 * EXPERTS * (g + 1) - (tiles == (2,)))
                sp.dma_start(out.rearrange("(i p) d -> p i d", p=TP)[:, tiles[0]:tiles[-1] + 1],
                             x_sb[:, tiles[0]:tiles[-1] + 1, :]).then_inc(sent, 16)
            sp.wait_ge(sent, 48)

        @block.gpsimd
        def _(pool):
            nc.gpsimd.memset(Wkr, 0.0).then_inc(clear_ready, 1)
            nc.gpsimd.memset(ident[:], 0.0)
            nc.gpsimd.memset(ident16[:], 0.0)
            nc.gpsimd.memset(ones[:], 1.0).then_inc(pool_seq, 1)
            pool.wait_ge(pool_seq, 1)
            for m in (ident, ident16):
                last = nc.gpsimd.affine_select(out=m[:], in_=m[:], compare_op=ALU.not_equal, fill=1.0, base=0,
                                               pattern=[[-1, 128]], channel_multiplier=1)
            last.then_inc(consts_ready, 1)
            pool.wait_ge(consts_ready, 1)
            for i in range(2):
                nc.gpsimd.memset(K_hi1[i][64:128], 0.0)
            nc.gpsimd.memset(Q_lo[64:128, :].bitcast(F32), 0.0).then_inc(clear_ready, 1)
            pool.wait_ge(clear_ready, 2)
            for i in range(2):
                last = nc.gpsimd.memset(K_hi1[i][64:65], -QS)
            last.then_inc(consts_ready, 1)
            pool.wait_ge(consts_ready, 2)

            def rope(n, c):
                b = 2 * n + c
                raw = kvf[0:KP, bass.ds(b * (KT_N * DC), KT_N * DC)].rearrange("p (t c) -> p t c", c=DC)
                cosv, sinv = (cs[:, i, :].rearrange("p (t c) -> p t c", c=DC) for i in range(2))
                pool.wait_ge(v_copied, 16 * b)
                pool.wait_ge(k_lo_ready, b)
                nc.gpsimd.tensor_tensor(roped[:], raw, cosv, ALU.mult)
                h = DC // 2
                nc.gpsimd.tensor_tensor(rot[:, :, 0:h], raw[:, :, h:DC], sinv[:, :, 0:h], ALU.mult)
                nc.gpsimd.tensor_tensor(rot[:, :, h:DC], raw[:, :, 0:h], sinv[:, :, h:DC], ALU.mult).then_inc(pool_seq, 1)
                pool.wait_ge(pool_seq, 1 + b)
                nc.gpsimd.tensor_tensor(roped[:], roped[:], rot[:], ALU.add).then_inc(rope_ready, 1)

            def low(n, c):
                b = 2 * n + c
                pool.wait_ge(k_hi_ready, b + 1)
                nc.gpsimd.tensor_tensor(K_split[:, :, DC:2 * DC], roped[:], K_split[:, :, 0:DC], ALU.subtract)\
                    .then_inc(k_lo_ready, 1)

            def add(n, c, i, j):
                b = 2 * n + c
                t = POOL_TILES[i]
                pool.wait_ge(exp_done, STEPS * b + 2 * t + j + 1)
                to = acc_pool[c % 2][:, j, :]
                if i == 1:
                    a = Pr[:, (2 * POOL_TILES[0] + j) % RING, :]
                else:
                    a = to
                    pool.wait_ge(pool_added, POOL_ADDS * b + 2 * (i - 1) + j - 1)
                nc.gpsimd.tensor_tensor(to, a, Pr[:, (2 * t + j) % RING, :], ALU.add).then_inc(pool_added, 1)

            pool.wait_ge(in_cs, 32)
            pool.wait_ge(in_kv1, 16)
            rope(0, 1)
            for p in range(PAIRS):
                pool.wait_ge(q_staged, p + 1)
                part = slice(SEQ * p, SEQ * p + SEQ)
                hi, lo, q = (v.rearrange("q (b n) -> q b n", b=BATCH)[:, 1:, part] for v in (stage_hi, stage_lo, stage_q))
                nc.gpsimd.tensor_tensor(lo, q, hi, ALU.subtract).then_inc(q_lo_staged, 1)
            low(0, 1)
            pool.wait_ge(in_kvs, 16 * (BATCH - 2))

            def body(n, c):
                if first(n, c):
                    rope(n, c + 2)
                for j in range(2):
                    add(n, c, 1, j)
                if has_rope(n, c) and not first(n, c):
                    rope(n, c + 2)
                for i in range(2, len(POOL_TILES)):
                    if i == len(POOL_TILES) - 1 and has_rope(n, c):
                        low(n, c + 2)
                    for j in range(2):
                        add(n, c, i, j)

            batches(pool, body)


        @block.scalar
        def _(act):
            def copy(to, of, **k):
                return nc.scalar.activation(to, of, ACT.Copy, **k)

            def k_hi(n, c):
                b = 2 * n + c
                act.wait_ge(rope_ready, b + 1)
                if c >= 1:
                    act.wait_ge(kt_made, 2 * b)
                copy(K_split[:, :, 0:DC], roped[:]).then_inc(k_hi_ready, 1)

            def kt(n, c, i):
                b = 2 * n + c
                act.wait_ge(kt_made, 2 * b + i + 1)
                of = AUX[i][:, :].bitcast(F16).rearrange("p (t k) -> p t k", k=128)[:, 0:6, 0:KP]
                copy(K_both[c % 2][:, 6 * i:6 * i + 6, :], of).then_inc(kt_ready, 1)

            def m_row(n, c, j, at):
                b = 2 * n + c
                act.wait_ge(m_made, 2 * b + j + 1)
                copy(Q_lo[64:65, bass.ds(b * ROWS + j * HALF, HALF)], at[j][64:65, 0:HALF]).then_inc(m_ready, 1)

            def w_high(n, c, i):
                b = 2 * n + c
                act.wait_ge(in_experts, 16 * (b + 1))
                part = EW // W_PARTS
                copy(W_hi_flat[:, bass.ds(b * EW + i * part, part)], raw_w[:, i * part:(i + 1) * part], scale=WS)\
                    .then_inc(w_hi_ready, 1)

            def save_ctx(n, c):
                b = 2 * n + c
                act.wait_ge(pv_done, KT_N * (b + 1))
                if c >= 1:
                    act.wait_ge(ctx_ready, b)
                copy(ctx_raw[:], PV[:, 0:HALF]).then_inc(ctx_saved, 1)

            def save_sums(n, c):
                b = 2 * n + c
                act.wait_ge(sum_made, b + 1)
                if c >= 1:
                    act.wait_ge(sum_thin, 32 * b)
                copy(sums[:], AUX[0][:, 0:HALF]).then_inc(sum_saved, 1)

            def norm(g):
                act.wait_ge(var_ready, g + 2)
                nc.scalar.activation(std[:, 2 * g:2 * g + 2], rstd[:, 2 * g:2 * g + 2], ACT.Sqrt).then_inc(std_ready, 1)

            def spread_x(g):
                act.wait_ge(xt_made, TT + g + 1)
                for to in (x_hi, xnT):
                    for i in range(2):
                        last = copy(to[:, :, TP * (2 * g + i):TP * (2 * g + i + 1)],
                                    AUX[g][:, 2 * TP * i:2 * TP * (i + 1)].rearrange("p (c n) -> p c n", c=2))
                last.then_inc(xt_act, 1)

            def gate_exp(g):
                act.wait_ge(logits_shifted, g + 1)
                nc.scalar.activation(gate["exp"], gate["shifted"], ACT.Exp).then_inc(gexp_done, 1)

            nc.scalar.preload_act_table(ACT.Sqrt)
            fold_to = [lambda p: (A1[:, p], banks[p][0:96, 0:256]), lambda p: (A2T[:, p], banks[p][:, 0:128]),
                       lambda p: (A2[:, p], banks[p][:, 0:128]), lambda p: (A3T[:, p], banks[p][:, 0:256]),
                       lambda p: (A3[:, p], banks[p][:, 0:256])]
            for s in range(5):
                for p in range(0, PAIRS, 2 if s < 4 else 1):
                    act.wait_ge(fold_made, PAIRS * s + p + 1)
                    to, of = fold_to[s](p)
                    if len(to.shape) == 3:
                        of = of.rearrange("p (c n) -> p c n", c=2)
                    copy(to, of).then_inc(fold_act, 1)
                if s == 0:
                    act.wait_ge(var_ready, 1)
                    nc.scalar.activation(std[:], rstd[:], ACT.Sqrt).then_inc(std_ready, 1)
                    nc.scalar.preload_act_table(ACT.Exp)
                if s == 4:
                    k_hi(0, 0)
                if s == 3:
                    for i in (0, 2):
                        act.wait_ge(xt_made, i + 1)
                        copy(xnT[:, :, TP * i:TP * i + TP], banks[i][:, 0:2 * TP].rearrange("p (c n) -> p c n", c=2))\
                            .then_inc(xt_act, 1)
            for p in range(PAIRS):
                act.wait_ge(q_made, p + 1)
                of = banks[2 + p % 6]
                for j in range(2):
                    for to in range(2):
                        last = copy(Q_hi[64 * to:64 * to + 64, HALF * j + SEQ * p:HALF * j + SEQ * p + SEQ],
                                    of[64 * j:64 * j + 64, 0:SEQ], scale=QS)
                last.then_inc(q0_hi_ready, 1)
                q, hi = (v.rearrange("q (b n) -> q b n", b=BATCH)[:, :, SEQ * p:SEQ * p + SEQ] for v in (stage_q, stage_hi))
                of = of[:, 0:TOK].rearrange("q (b s) -> q b s", b=BATCH)
                copy(q, of, scale=QS).then_inc(q_copied, 1)
                copy(hi[:, 1:], of[:, 1:], scale=QS).then_inc(q_staged, 1)
                if p == KT_AFTER:
                    for i in range(2):
                        kt(0, 0, i)
            k_hi(0, 1)
            for p in range(PAIRS):
                act.wait_ge(vf_made, p + 1)
                copy(VF[:, p], VF_BANKS[p % 4][:, 0:DM]).then_inc(vf_ready, 1)
            for j in range(2):
                m_row(0, 0, j, MX)

            def body(n, c):
                b = 2 * n + c
                for k in range(STEPS):
                    act.wait_ge(st_made, STEPS * b + k + 1)
                    if not (first(n, c) and k < RING):
                        bb, kk = (b, k - RING) if k >= RING else (b - 1, k - RING + STEPS)
                        act.wait_ge(pv_done, KT_N * bb + kk // 2 + 1)
                        t, j = kk // 2, kk % 2
                        if t in POOL_TILES:
                            act.wait_ge(pool_added, POOL_ADDS * bb + adds_after(POOL_TILES, t, j))
                        else:
                            act.wait_ge(dve_added, DVE_ADDS * bb + adds_after(DVE_TILES, t, j))
                    nc.scalar.activation(Pr[:, k % RING, :], ST[k % 3][0:KP, 0:HALF], ACT.Exp, scale=1.0 / QS)\
                        .then_inc(exp_done, 1)
                    if k < 2 and has_next(n, c) and not first(n, c):
                        kt(n, c + 1, k)
                    if k == 1 and not first(n, c):
                        save_ctx(n, c - 1)
                    if k == 5 and not first(n, c):
                        save_sums(n, c - 1)
                    if k in high_at(c):
                        w_high(n, c, high_at(c).index(k))
                    if k == 13 and has_rope(n, c):
                        k_hi(n, c + 2)
                    if k in (21, 22) and has_next(n, c):
                        m_row(n, c + 1, k - 21, AUX)
                    if c == 6 and k == NORM_AT:
                        norm(0)
                    if c == 7:
                        if k == 12:
                            spread_x(0)
                        if k == 18:
                            gate_exp(0)

            batches(act, body)
            save_ctx(0, 7)
            for u in range(2 * EXPERTS):
                act.wait_ge(up_made, u + 1)
                if u >= 1:
                    act.wait_ge(h_made, u)
                nc.scalar.activation(silu_sb, banks[2 * (u % UPS)][:, 0:4 * TP], ACT.Silu, scale=1.0 / WS).then_inc(silu_done, 1)
                if u == 0:
                    save_sums(0, 7)
                act.wait_ge(h_made, u + 1)
                if u >= 2:
                    act.wait_ge(down_made, u - 1)
                copy(h_hi[u % 2].rearrange("p c n -> p (c n)"), h_sb).then_inc(h_hi_ready, 1)
                if u == TAIL_AT + 1:
                    norm(1)
                if u == EXPERTS - 2:
                    spread_x(1)
                if u == EXPERTS:
                    gate_exp(1)

        @block.vector
        def _(dve):
            chain = [0]

            def link(ins):
                chain[0] += 1
                ins.then_inc(dve_seq, 1)
                dve.wait_ge(dve_seq, chain[0])

            def norm(tiles):
                lo, hi = tiles[0], tiles[-1] + 1
                for i in tiles:
                    last = nc.vector.bn_stats(stats[:, i, :], x_sb[:, i, :])
                link(last)
                for i in tiles:
                    last = nc.vector.bn_aggr(mv[:, i, :], stats[:, i, :])
                link(last)
                nc.vector.tensor_scalar(rstd[:, lo:hi], mv[:, lo:hi, 1], LN_EPS, None, ALU.add).then_inc(var_ready, 1)

            def normalise(tiles, k, xn):
                lo, hi = tiles[0], tiles[-1] + 1
                dve.wait_ge(std_ready, k + 1)
                link(nc.vector.reciprocal(rstd[:, lo:hi], std[:, lo:hi]))
                for i in tiles:
                    last = nc.vector.tensor_scalar(xn[:, i, :], x_sb[:, i, :], mv[:, i, 0:1], rstd[:, i:i + 1],
                                                   ALU.subtract, ALU.mult)
                last.then_inc(xn_ready, 1)

            fold_to = [lambda p: (A1[:, p], banks[p][0:96, 0:256]), lambda p: (A2T[:, p], banks[p][:, 0:128]),
                       lambda p: (A2[:, p], banks[p][:, 0:128]), lambda p: (A3T[:, p], banks[p][:, 0:256])]
            for s in range(4):
                for p in range(1, PAIRS, 2):
                    dve.wait_ge(fold_made, PAIRS * s + p + 1)
                    to, of = fold_to[s](p)
                    if len(to.shape) == 3:
                        of = of.rearrange("p (c n) -> p c n", c=2)
                    nc.vector.tensor_copy(to, of).then_inc(fold_dve, 1)
                if s == 0:
                    dve.wait_ge(in_x, 16)
                    norm(range(TT))
                if s == 2:
                    normalise(range(TT), 0, xn1)
                if s == 3:
                    for i in (1, 3):
                        dve.wait_ge(xt_made, i + 1)
                        nc.vector.tensor_copy(xnT[:, :, TP * i:TP * i + TP],
                                              banks[i][:, 0:2 * TP].rearrange("p (c n) -> p c n", c=2)).then_inc(xt_dve, 1)

            dve.wait_ge(in_cs, 32)
            dve.wait_ge(in_kv0, 16)
            raw, cosv, sinv = (v.rearrange("p (t c) -> p t c", c=DC) for v in (kv[0:KP, 0, :], cs[:, 0, :], cs[:, 1, :]))
            h = DC // 2
            nc.vector.tensor_tensor(roped[:], raw, cosv, ALU.mult)
            nc.vector.tensor_tensor(rot[:, :, 0:h], raw[:, :, h:DC], sinv[:, :, 0:h], ALU.mult)
            link(nc.vector.tensor_tensor(rot[:, :, h:DC], raw[:, :, 0:h], sinv[:, :, h:DC], ALU.mult))
            nc.vector.tensor_tensor(roped[:], roped[:], rot[:], ALU.add).then_inc(rope_ready, 1)
            dve.wait_ge(k_hi_ready, 1)
            nc.vector.tensor_tensor(K_split[:, :, DC:2 * DC], roped[:], K_split[:, :, 0:DC], ALU.subtract).then_inc(k_lo_ready, 1)

            def reduce_chunk(n, c, i, of=None):
                b = 2 * n + c
                dve.wait_ge(mx_made, CHUNKS * b + i + 1)
                r, q = divmod(i if of is None else of, MXQ)
                nc.vector.tensor_reduce(mx_part[:, r, q:q + 1], MX[(c + i) % 2][:, 0:MXC],
                                        X_AXIS, ALU.max).then_inc(mx_read, 1)

            def maxima(n, c):
                b = 2 * n + c
                dve.wait_ge(mx_read, CHUNKS * (b + 1))
                nc.vector.tensor_reduce(mx[:], mx_part[:], X_AXIS, ALU.max).then_inc(mx_whole, 1)
                dve.wait_ge(mx_whole, b + 1)
                nc.vector.tensor_scalar(mx16[:], mx[:], 1.0 / QS, None, ALU.mult).then_inc(mx16_ready, 1)

            def add(n, c, t, j):
                b = 2 * n + c
                i = DVE_TILES.index(t)
                if i == 0:
                    return
                dve.wait_ge(exp_done, STEPS * b + 2 * t + j + 1)
                to = acc_dve[c % 2][:, j, :]
                if i == 1:
                    a = Pr[:, (2 * DVE_TILES[0] + j) % RING, :]
                else:
                    a = to
                    dve.wait_ge(dve_added, DVE_ADDS * b + 2 * (i - 1) + j - 1)
                nc.vector.tensor_tensor(to, a, Pr[:, (2 * t + j) % RING, :], ALU.add).then_inc(dve_added, 1)

            def merge(n, c):
                b = 2 * n + c
                dve.wait_ge(pool_added, POOL_ADDS * (b + 1))
                dve.wait_ge(dve_added, DVE_ADDS * (b + 1))
                nc.vector.tensor_tensor(acc_dve[c % 2], acc_dve[c % 2], acc_pool[c % 2], ALU.add).then_inc(sum_merged, 1)

            def w_low(n, c, i):
                b = 2 * n + c
                dve.wait_ge(w_hi_ready, W_PARTS * b + i + 1)
                part = EW // W_PARTS
                at = bass.ds(b * EW + i * part, part)
                nc.vector.scalar_tensor_tensor(W_lo_flat[:, at], raw_w[:, i * part:(i + 1) * part], WS, W_hi_flat[:, at],
                                               ALU.mult, ALU.subtract).then_inc(w_lo_ready, 1)

            def reciprocals(n, c):
                b = 2 * n + c
                dve.wait_ge(sum_thin, 32 * (b + 1))
                nc.vector.reciprocal(recip_thin[:], sums_thin[:]).then_inc(recip_done, 1)

            def context(n, c):
                b = 2 * n + c
                dve.wait_ge(recip_wide, 32 * (b + 1))
                dve.wait_ge(ctx_saved, b + 1)
                at = SEQ * (c % 2)
                nc.vector.tensor_tensor(ctxT[:, :, at:at + SEQ], ctx_raw[:].rearrange("p (h s) -> p h s", h=PAIRS),
                                        recip[:].rearrange("p (h s) -> p h s", h=PAIRS), ALU.mult).then_inc(ctx_ready, 1)

            def residual(tile):
                dve.wait_ge(proj_made, tile + 1)
                at = x_flat[:, bass.ds(tile * DM, DM)]
                nc.vector.tensor_tensor(at, AUX[1][0:TP, 0:DM], at, ALU.add).then_inc(x1_ready, 1)

            def first_rows(i):
                for q in range(MXQ):
                    reduce_chunk(0, 0, MXQ * i + q, MXQ * FIRST_ORDER[i] + q)

            x_flat = x_sb[:, :, :].rearrange("p i d -> p (i d)")
            for p in range(PAIRS):
                if p >= 3:
                    first_rows(p - 3)
                dve.wait_ge(q0_hi_ready, p + 1)
                dve.wait_ge(q_copied, p + 1)
                for j in range(2):
                    part = slice(HALF * j + SEQ * p, HALF * j + SEQ * p + SEQ)
                    last = nc.vector.tensor_tensor(Q_lo[0:64, part], stage_q[64 * j:64 * j + 64, SEQ * p:SEQ * p + SEQ],
                                                   Q_hi[64 * j:64 * j + 64, part], ALU.subtract)
                last.then_inc(q0_lo_ready, 1)
            first_rows(5)
            first_rows(6)
            maxima(0, 0)
            for i in range(2):
                dve.wait_ge(kt_made, 2 + i + 1)
                of = AUX[i][:, :].bitcast(F16).rearrange("p (t k) -> p t k", k=128)[:, 0:6, 0:KP]
                nc.vector.tensor_copy(K_both[1][:, 6 * i:6 * i + 6, :], of).then_inc(kt_ready, 1)

            def wide(v):
                return v.unsqueeze(2).to_broadcast([TP, 2, ROUTED])

            def shift_logits(g):
                dve.wait_ge(gate_made, g + 1)
                logit = banks[7][0:TP, 0:32].rearrange("p (i e) -> p i e", i=2)[:, :, 0:ROUTED]
                link(nc.vector.tensor_tensor(gate["logit"], logit, gb[:], ALU.add))
                link(nc.vector.tensor_reduce(gate1["max"], gate["logit"], X_AXIS, ALU.max))
                nc.vector.tensor_tensor(gate["shifted"], gate["logit"], wide(gate1["max"]), ALU.subtract).then_inc(logits_shifted, 1)

            def gate_order(g):
                dve.wait_ge(gexp_done, g + 1)
                link(nc.vector.tensor_reduce(gate1["sum"], gate["exp"], X_AXIS, ALU.add))
                link(nc.vector.reciprocal(gate1["rsum"], gate1["sum"]))
                link(nc.vector.tensor_tensor(gate["prob"], gate["exp"], wide(gate1["rsum"]), ALU.mult))
                link(nc.vector.tensor_tensor(gate["biased"], gate["prob"], bi[:], ALU.add))
                other = gate["biased"].unsqueeze(2).to_broadcast([TP, 2, ROUTED, ROUTED])
                own = gate["biased"].unsqueeze(3).to_broadcast([TP, 2, ROUTED, ROUTED])
                nc.vector.tensor_tensor(above, other, own, ALU.is_gt)
                link(nc.vector.tensor_tensor(equal, other, own, ALU.is_equal))
                link(nc.vector.tensor_tensor(equal, equal, bef[:], ALU.mult))
                link(nc.vector.tensor_tensor(above, above, equal, ALU.add))

            def gate_weights(g):
                link(nc.vector.tensor_reduce(gate["rank"], above, X_AXIS, ALU.add))
                link(nc.vector.tensor_scalar(gate["rank"], gate["rank"], TOP_K - 0.5, None, ALU.is_lt))
                link(nc.vector.tensor_tensor(gate["picked"], gate["prob"], gate["rank"], ALU.mult))
                link(nc.vector.tensor_reduce(gate1["wsum"], gate["picked"], X_AXIS, ALU.add))
                link(nc.vector.reciprocal(gate1["rwsum"], gate1["wsum"]))
                link(nc.vector.tensor_scalar(gate1["rwsum"], gate1["rwsum"], 1.0 / (WS * HS), None, ALU.mult))
                link(nc.vector.tensor_tensor(weight[:, 2 * g:2 * g + 2], gate["picked"], wide(gate1["rwsum"]), ALU.mult))

            def x_low(g):
                dve.wait_ge(xt_act, 2 + g + 1)
                for i in range(2):
                    part = slice(TP * (2 * g + i), TP * (2 * g + i + 1))
                    last = nc.vector.tensor_tensor(x_lo[:, :, part],
                                                   AUX[g][:, 2 * TP * i:2 * TP * (i + 1)].rearrange("p (c n) -> p c n", c=2),
                                                   x_hi[:, :, part], ALU.subtract)
                last.then_inc(x_lo_ready, 1)

            def combine(u):
                g, e = divmod(u, EXPERTS)
                dve.wait_ge(down_made, u + 1)
                for i in range(2):
                    t = 2 * g + i
                    of = out_bank(u)[0:TP, DM * i:DM * i + DM]
                    if e == 0:
                        nc.vector.scalar_tensor_tensor(x_sb[:, t, :], of, 1.0 / (WS * HS), x_sb[:, t, :],
                                                       ALU.mult, ALU.add).then_inc(y_ready, 1)
                    else:
                        dve.wait_ge(y_ready, 2 * (u - 1) + i + 1)
                        nc.vector.scalar_tensor_tensor(x_sb[:, t, :], of, weight[:, t, e - 1:e], x_sb[:, t, :],
                                                       ALU.mult, ALU.add).then_inc(y_ready, 1)

            def body(n, c):
                for k in range(STEPS + 2):
                    if has_next(n, c):
                        for i in max_chunks_at(k):
                            reduce_chunk(n, c + 1, i)
                    if k >= 2 and (k - 2) // 2 in DVE_TILES:
                        add(n, c, (k - 2) // 2, k % 2)
                    if k == 9 and not first(n, c):
                        reciprocals(n, c - 1)
                    if k in low_at(c):
                        w_low(n, c, low_at(c).index(k))
                    if k == 15 and not first(n, c):
                        context(n, c - 1)
                    if k == 19 and c % 2 == 0 and not first(n, c):
                        residual(n + c // 2 - 1)
                    if k == 19 and has_next(n, c):
                        maxima(n, c + 1)
                    if c == 6 and k == 1:
                        dve.wait_ge(x1_ready, 2)
                        norm((0, 1))
                    if c == 7:
                        if k == 6:
                            normalise((0, 1), 1, xn2)
                        if k == 15:
                            x_low(0)
                        if k == 19:
                            shift_logits(0)
                merge(n, c)

            batches(dve, body)
            gate_order(0)
            gate_weights(0)
            for u in range(2 * EXPERTS):
                dve.wait_ge(silu_done, u + 1)
                if u >= 1:
                    dve.wait_ge(h_hi_ready, u)
                    dve.wait_ge(h_lo_ready, u)
                nc.vector.scalar_tensor_tensor(h_sb, banks[2 * (u % UPS) + 1][:, 0:4 * TP], HS / WS, silu_sb,
                                               ALU.mult, ALU.mult).then_inc(h_made, 1)
                if u == 1:
                    reciprocals(0, 7)
                if u >= 2:
                    combine(u - 2)
                dve.wait_ge(h_hi_ready, u + 1)
                nc.vector.tensor_tensor(h_lo[u % 2].rearrange("p c n -> p (c n)"), h_sb,
                                        h_hi[u % 2].rearrange("p c n -> p (c n)"), ALU.subtract).then_inc(h_lo_ready, 1)
                if u == TAIL_AT:
                    context(0, 7)
                if u == TAIL_AT + 1:
                    residual(TT - 1)
                    dve.wait_ge(x1_ready, TT)
                    norm((2, 3))
                if u == TAIL_AT + 2:
                    normalise((2, 3), 2, xn2)
                if u == EXPERTS - 2:
                    x_low(1)
                if u == EXPERTS:
                    shift_logits(1)
                if u == EXPERTS + 1:
                    gate_order(1)
                if u == EXPERTS + 2:
                    gate_weights(1)
            combine(2 * EXPERTS - 2)
            combine(2 * EXPERTS - 1)

        @block.tensor
        def _(pe):
            def folded(s, p):
                if s == 4:
                    pe.wait_ge(fold_act, 4 * s + p + 1)
                else:
                    pe.wait_ge(fold_act if p % 2 == 0 else fold_dve, 4 * s + p // 2 + 1)

            pe.wait_ge(consts_ready, 1)
            for i in range(WARM_UP):
                nc.tensor.matmul(banks[7][:, 0:128], ident[:], ident[:], start=True, stop=True)
            pe.wait_ge(in_fold1, 48)
            for p in range(PAIRS):
                for c in range(2):
                    last = nc.tensor.matmul(banks[p][0:96, 128 * c:128 * c + 128], Wqr[:, p, 96 * c:96 * c + 96],
                                            Wkr[:, p, :], start=True, stop=True)
                last.then_inc(fold_made, 1)
            for p in range(PAIRS):
                if p % 4 == 0:
                    pe.wait_ge(in_fold2[p // 4], 16)
                folded(0, p)
                for c in range(2):
                    for j in range(2):
                        last = nc.tensor.matmul(banks[p][64 * j:64 * j + 64, 0:128], A1[:, p, c, 64 * j:64 * j + 64],
                                                Kcq[:, j, p, DK * c:DK * c + DK], start=(c == 0), stop=(c == 1))
                last.then_inc(fold_made, 1)
            for p in range(PAIRS):
                folded(1, p)
                nc.tensor.transpose(banks[p][:, 0:128], A2T[:, p, :], ident[:]).then_inc(fold_made, 1)
            for p in range(PAIRS):
                if p % 4 == 0:
                    pe.wait_ge(in_wq[p // 4], 32)
                folded(2, p)
                for j in range(2):
                    last = nc.tensor.matmul(banks[p][64 * j:64 * j + 64, 0:DM], A2[:, p, 64 * j:64 * j + 64],
                                            Wq[:, p + PAIRS * j, :], start=True, stop=True)
                last.then_inc(fold_made, 1)
            pe.wait_ge(xn_ready, 1)
            for i in range(TT):
                folded(3, i)
                for c in range(2):
                    last = nc.tensor.transpose(banks[i][:, TP * c:TP * c + TP], xn1[:, i, 128 * c:128 * c + 128],
                                               ident[0:TP, 0:TP])
                last.then_inc(xt_made, 1)
            for p in range(PAIRS):
                folded(3, p)
                if p < TT:
                    pe.wait_ge(xt_act if p % 2 == 0 else xt_dve, p // 2 + 1)
                for c in range(2):
                    last = nc.tensor.transpose(banks[p][:, 128 * c:128 * c + 128], A3T[:, p, 128 * c:128 * c + 128], ident[:])
                last.then_inc(fold_made, 1)
            def kt(n, c, i):
                b = 2 * n + c
                if i == 0:
                    pe.wait_ge(k_lo_ready, b + 1)
                for t in range(6 * i, 6 * i + 6):
                    to = AUX[t // 6][:, :].bitcast(F16)[:, 128 * (t % 6):128 * (t % 6) + KP]
                    last = nc.tensor.transpose(to, K_split[:, t, :], ident16[0:KP, 0:KP])
                last.then_inc(kt_made, 1)

            def max_chunk(n, c, i, of=None):
                b = 2 * n + c
                if i == 0:
                    pe.wait_ge(kt_ready, 2 * (b + 1))
                if not (c == 0 and i < 2):
                    pe.wait_ge(mx_read, CHUNKS * b + i - 1)
                r, q = divmod(i if of is None else of, MXQ)
                nc.tensor.matmul(MX[(c + i) % 2][:, 0:MXC], Q_hi[:, bass.ds(b * ROWS + 128 * r, 128)],
                                 K_both[c % 2][:, 4 * q:4 * q + 4, :].rearrange("p t k -> p (t k)"),
                                 start=True, stop=True).then_inc(mx_made, 1)

            def m_row(n, c, at):
                b = 2 * n + c
                pe.wait_ge(mx16_ready, b + 1)
                for j in range(2):
                    for r in range(RT):
                        lo, hi = max(128 * r, HALF * j), min(128 * r + 128, HALF * j + HALF)
                        if lo < hi:
                            last = nc.tensor.matmul(at[j][64:65, lo - HALF * j:hi - HALF * j], mx16[:, r:r + 1],
                                                    ident16[:, lo - 128 * r:hi - 128 * r], start=True, stop=True)
                    last.then_inc(m_made, 1)

            def pv(n, c, t):
                b = 2 * n + c
                pe.wait_ge(exp_done, STEPS * b + 2 * t + 2)
                if t == 0:
                    pe.wait_ge(v_copied, 16 * (b + 1))
                    if c >= 1:
                        pe.wait_ge(ctx_saved, b)
                for j in range(2):
                    last = nc.tensor.matmul(PV[64 * j:64 * j + 64, 0:HALF], V[c % 2][:, t, :], Pr[:, (2 * t + j) % RING, :],
                                            start=(t == 0), stop=(t == KT_N - 1))
                last.then_inc(pv_done, 1)

            def row_sums(n, c):
                b = 2 * n + c
                pe.wait_ge(sum_merged, b + 1)
                for j in range(2):
                    last = nc.tensor.matmul(AUX[0][64 * j:64 * j + 64, 0:HALF], ones[0:KP, :], acc_dve[c % 2][:, j, :],
                                            start=True, stop=True)
                last.then_inc(sum_made, 1)

            def project(n, c, parts):
                b = 2 * n + c
                if parts[0] == 0:
                    pe.wait_ge(ctx_ready, b + 1)
                for p in parts:
                    last = nc.tensor.matmul(AUX[1][0:TP, 0:DM], ctxT[:, p, :], VF[:, p, :], start=(p == 0), stop=(p == PAIRS - 1))
                if parts[-1] == PAIRS - 1:
                    last.then_inc(proj_made, 1)

            def first_rows(i, q):
                r = FIRST_ORDER[i]
                if q == 0:
                    heads = range(128 * r // SEQ, (128 * r + 127) // SEQ + 1)
                    pe.wait_ge(q0_hi_ready, max(h % PAIRS for h in heads) + 1)
                max_chunk(0, 0, MXQ * i + q, MXQ * r + q)

            for p in range(PAIRS):
                folded(4, min(p + 2, PAIRS - 1))
                if p == KT_AFTER + 1:
                    folded(4, PAIRS - 1)
                    kt(0, 0, 0)
                    kt(0, 0, 1)
                if p in (4, 5):
                    pe.wait_ge(kt_ready, p - 3)
                if p >= 6:
                    pe.wait_ge(q_staged, p - 5)
                for c in range(2):
                    last = nc.tensor.matmul(banks[2 + p % 6][:, 0:TOK], A3[:, p, c, :], xnT[:, c, :],
                                            start=(c == 0), stop=(c == 1))
                    if p >= 3 and c == 0:
                        first_rows(p - 3, 0)
                last.then_inc(q_made, 1)
                if p >= 3:
                    first_rows(p - 3, 1)
                    first_rows(p - 3, 2)
            pe.wait_ge(in_vfold, 32)
            for p in range(PAIRS):
                if p < 4:
                    pe.wait_ge(q_staged, (3, 4, 7, 8)[p])
                else:
                    pe.wait_ge(vf_ready, p - 3)
                for j in range(2):
                    last = nc.tensor.matmul(VF_BANKS[p % 4][64 * j:64 * j + 64, 0:DM], Kckv[:, p + PAIRS * j, :],
                                            WoT[:, p + PAIRS * j, :], start=True, stop=True)
                last.then_inc(vf_made, 1)
                if p < 6:
                    first_rows(5 + p // 3, p % 3)
            pe.wait_ge(q_staged, 6)
            m_row(0, 0, MX)
            kt(0, 1, 0)
            kt(0, 1, 1)
            pe.wait_ge(consts_ready, 2)
            pe.wait_ge(q0_lo_ready, PAIRS)
            pe.wait_ge(vf_ready, PAIRS)

            def transpose_x(g):
                pe.wait_ge(xn_ready, g + 2)
                if g == 1:
                    pe.wait_ge(x1_ready, TT)
                for i in range(2):
                    for c in range(2):
                        last = nc.tensor.transpose(AUX[g][:, TP * (2 * i + c):TP * (2 * i + c) + TP],
                                                   xn2[:, 2 * g + i, 128 * c:128 * c + 128], ident[0:TP, 0:TP])
                last.then_inc(xt_made, 1)

            def gate_logits(g):
                if g == 0:
                    pe.wait_ge(in_gate, 64)
                pe.wait_ge(xt_act, 2 + g + 1)
                if g == 0:
                    pe.wait_ge(x1_ready, 3)
                else:
                    pe.wait_ge(x_lo_ready, 2)
                for i in range(2):
                    for c in range(2):
                        last = nc.tensor.matmul(banks[7][0:TP, 16 * i:16 * i + ROUTED],
                                                xnT[:, c, TP * (2 * g + i):TP * (2 * g + i + 1)], gw[:, c, :],
                                                start=(c == 0), stop=(c == 1))
                last.then_inc(gate_made, 1)

            def up(u):
                g, e = divmod(u, EXPERTS)
                if u >= UPS:
                    pe.wait_ge(h_made, u - UPS + 1)
                at = slice(2 * TP * g, 2 * TP * (g + 1))
                for w in range(2):
                    for h in range(2):
                        terms = [(W, X, c) for c in range(2) for W, X in ((W_hi, x_hi), (W_hi, x_lo), (W_lo, x_hi))]
                        for n, (W, X, c) in enumerate(terms):
                            o = DM * (2 * w + c) + 128 * h
                            last = nc.tensor.matmul(banks[2 * (u % UPS) + w][:, 2 * TP * h:2 * TP * (h + 1)],
                                                    W[:, e, o:o + 128], X[:, c, at], start=(n == 0), stop=(n == len(terms) - 1))
                last.then_inc(up_made, 1)

            def down(u):
                g, e = divmod(u, EXPERTS)
                pe.wait_ge(h_lo_ready, u + 1)
                if u >= 1:
                    pe.wait_ge(y_ready, 2 * (u - 1 if u > TWO_OUT else u))
                for i in range(2):
                    terms = [(X, W, c) for c in range(2) for X, W in ((h_hi, W_hi), (h_hi, W_lo), (h_lo, W_hi))]
                    for n, (X, W, c) in enumerate(terms):
                        o = 4 * DM + DM * c
                        last = nc.tensor.matmul(out_bank(u)[0:TP, DM * i:DM * i + DM], X[u % 2][:, c, TP * i:TP * i + TP],
                                                W[:, e, o:o + DM], start=(n == 0), stop=(n == len(terms) - 1))
                last.then_inc(down_made, 1)

            def body(n, c):
                b = 2 * n + c
                for k in range(STEPS):
                    t, j = divmod(k, 2)
                    rows = bass.ds(b * ROWS + HALF * j, HALF)
                    if k < 2:
                        pe.wait_ge(m_ready, 2 * b + k + 1)
                    if k == 0:
                        pe.wait_ge(k_hi1_copied, 16 * (b + 1))
                    if not (first(n, c) and k < 3):
                        pe.wait_ge(exp_done, STEPS * b + k - 2)
                    nc.tensor.matmul(ST[k % 3][0:KP, 0:HALF], K_both[c % 2][:, t, :], Q_hi[:, rows], start=True, stop=False)
                    nc.tensor.matmul(ST[k % 3][0:KP, 0:HALF], K_hi1[c % 2][:, t, :], Q_lo[:, rows], start=False, stop=True)\
                        .then_inc(st_made, 1)
                    if first(n, c) and k == 3:
                        pe.wait_ge(q1_spread, 4 * 16)
                    if first(n, c) and k == STEPS - 1:
                        pe.wait_ge(q_spread, 6 * 16)
                    if has_next(n, c):
                        if k < 2 and not first(n, c):
                            kt(n, c + 1, k)
                        for i in max_chunks_at(k)[:1]:
                            max_chunk(n, c + 1, i)
                    if k == 1 and not first(n, c):
                        pv(n, c - 1, KT_N - 1)
                    if j == 1 and t >= 1:
                        pv(n, c, t - 1)
                    if has_next(n, c):
                        for i in max_chunks_at(k)[1:]:
                            max_chunk(n, c + 1, i)
                    if k == 4 and not first(n, c):
                        if has_next(n, c):
                            pe.wait_ge(kt_ready, 2 * (b + 2))
                        row_sums(n, c - 1)
                    if k in (17, 18) and c % 2 == 0 and not first(n, c):
                        project(n, c - 1, range(4 * (k - 17), 4 * (k - 16)))
                    if c == 7 and k == 10:
                        pe.wait_ge(sum_saved, 7)
                        transpose_x(0)
                    if c == 7 and k == 16:
                        gate_logits(0)
                    if k == 21 and has_next(n, c):
                        if not first(n, c):
                            pe.wait_ge(sum_saved, b)
                        m_row(n, c + 1, AUX)

            batches(pe, body)
            pv(0, 7, KT_N - 1)
            pe.wait_ge(w_lo_ready, W_PARTS * EXPERTS)
            pe.wait_ge(x_lo_ready, 1)
            up(0)
            row_sums(0, 7)
            up(1)
            pe.wait_ge(ctx_saved, BATCH)
            pe.wait_ge(sum_saved, BATCH)
            for u in range(2 * EXPERTS):
                if u == TAIL_AT:
                    project(0, 7, range(PAIRS))
                if u == EXPERTS - 3:
                    transpose_x(1)
                if u == EXPERTS - 2:
                    pe.wait_ge(x_lo_ready, 2)
                if u + 2 < 2 * EXPERTS:
                    up(u + 2)
                if u == EXPERTS - 2:
                    gate_logits(1)
                down(u)


def rotary_tables():
    inv_freq = np.float32(1.0) / np.float32(10000.0) ** (np.arange(0, DC, 2, dtype=np.float32) / np.float32(DC))
    angle = np.arange(KEYS, dtype=np.float32)[:, None] * inv_freq[None, :]
    sin, cos = (np.repeat(f(angle), 2, axis=-1).astype(np.float32) for f in (np.sin, np.cos))
    sin[:, :DC // 2] *= -1
    return [np.ascontiguousarray(a.reshape(KP, KT_N * DC)) for a in (cos, sin)]


def kernel(**inputs):
    import concourse.bacc as bacc
    from concourse.bass_utils import run_bass_kernel_spmd

    a = {k.replace("L0_", ""): np.asarray(v) for k, v in inputs.items()}
    lay = np.ascontiguousarray

    def by_pair(w):
        return lay(w.reshape(2, PAIRS, w.shape[1], w.shape[2]).transpose(0, 2, 1, 3).reshape(2 * w.shape[1], PAIRS, -1))

    up = np.stack([np.concatenate([a["ffn_Ws1"][None], a["ffn_W1"]]), np.concatenate([a["ffn_Wsg"][None], a["ffn_Wg"]])], 1)
    down = np.concatenate([a["ffn_Ws2"][None], a["ffn_W2"]])
    cos, sin = rotary_tables()
    arrays = {
        "x": a["x"].reshape(TOK, DM),
        "ctx": a["ctx_512"],
        "wqr": by_pair(a["xattn_W_qr"].transpose(0, 2, 1)),
        "wkr": by_pair(a["xattn_W_kr"].transpose(0, 2, 1)),
        "kcq": lay(a["xattn_w_kc_q"].reshape(HEADS, DK, 2, 96).transpose(3, 0, 2, 1).reshape(96, 2, PAIRS, 2 * DK)),
        "wq": a["xattn_Wq"],
        "kckv": lay(a["xattn_w_kc_kv"].transpose(1, 0, 2)),
        "wo": lay(a["xattn_Wo"].reshape(DM, HEADS, DK).transpose(2, 1, 0)),
        "w_exp": lay(np.concatenate([up.reshape(EXPERTS, 2, 2, 128, HID), down.reshape(EXPERTS, 1, 2, 128, DM)], 1)
                     .transpose(0, 3, 1, 2, 4).reshape(EXPERTS, 128, EW)),
        "gate_w": lay(a["ffn_gate_w"].reshape(2, 128, ROUTED).transpose(1, 0, 2)),
        "gate_b": lay(np.broadcast_to(a["ffn_gate_b"], (TP, 2, ROUTED))),
        "biases": lay(np.broadcast_to(a["ffn_biases"], (TP, 2, ROUTED))),
        "before": lay(np.broadcast_to(np.tril(np.ones((ROUTED, ROUTED), np.float32), -1), (TP, 2, ROUTED, ROUTED))),
        "cos": cos,
        "sin": sin,
    }
    nc = bacc.Bacc("TRN2", target_bir_lowering=False, num_devices=1)
    args = [nc.dram_tensor(f"in_{n}", v.shape, mybir.dt.from_np(v.dtype), kind="ExternalInput").ap() for n, v in arrays.items()]
    out = nc.dram_tensor("out", (TOK, DM), F32, kind="ExternalOutput").ap()
    build(nc, *args, out)
    r = run_bass_kernel_spmd(nc, [{f"in_{n}": v for n, v in arrays.items()}], core_ids=[0])
    return r.results[0]["out"].reshape(BATCH, SEQ, DM)
```
